# Optimizing a Trainium2 kernel written in Bass

```python
import numpy as np
import jax
import jax.numpy as jnp

def _softmax(x, axis=-1):
    return jax.nn.softmax(x, axis=axis)

def _gelu(x):
    return jax.nn.gelu(x, approximate=True)

def _silu(x):
    return jax.nn.silu(x)

def _sigmoid(x):
    return jax.nn.sigmoid(x)

def _layernorm(x, axis=-1, eps=1e-05):
    m = jnp.mean(x, axis=axis, keepdims=True)
    v = jnp.var(x, axis=axis, keepdims=True)
    return (x - m) / jnp.sqrt(v + eps)

def _scatter_add(tgt, idx, src, axis=0):
    return tgt.at[idx].add(src)

def _segment_sum(src, seg, n):
    return jax.ops.segment_sum(src, seg, n)
kernel_name = 'mk_xattn_seq_d1_seqx_r8_61e8bb'

def setup_inputs(seed: int=0):
    np.random.seed(seed)
    _w = jnp.asarray

    def _rec_inputs():
        import jax
        import jax.numpy as jnp
        _rk = jax.random.key(seed)
        x = 7.22e-05 + 1 * jax.random.normal(jax.random.fold_in(_rk, 1), (8, 256, 256), jnp.float32)
        _lenS = 256 - jax.random.randint(jax.random.fold_in(_rk, 7), (8,), 0, max(1, 256 // 4) + 1, jnp.int32)
        _lenS2 = 1601 - jax.random.randint(jax.random.fold_in(_rk, 8), (8,), 0, max(1, 1601 // 4) + 1, jnp.int32)
        _ctx_2048P = jax.random.normal(jax.random.fold_in(_rk, 11), (8, 16, 256), jnp.float32)
        _ctx_2048c = jax.random.dirichlet(jax.random.fold_in(_rk, 511), 0.3 * jnp.ones((16,), jnp.float32), (8, 1601))
        _ctx_2048t = jnp.einsum('bsk,bkd->bsd', _ctx_2048c, _ctx_2048P)
        _ctx_2048t = _ctx_2048t * jax.lax.rsqrt(jnp.mean(jnp.square(_ctx_2048t)) + 1e-12) * 0.953939
        ctx_2048 = 2.81802e-05 + 1.00001 * (_ctx_2048t + 0.3 * jax.random.normal(jax.random.fold_in(_rk, 611), (8, 1601, 256), jnp.float32))
        _validS = jnp.arange(256)[None, :] < _lenS[:, None]
        _validS2 = jnp.arange(1601)[None, :] < _lenS2[:, None]
        _causal = jnp.tril(jnp.ones((256, 256), dtype=bool))
        mask_BxS2_bf1 = jnp.ones((8, 1601), dtype=bool)
        return (x, ctx_2048, mask_BxS2_bf1)
    x, ctx_2048, mask_BxS2_bf1 = _rec_inputs()

    def _L0_xattn_setup():
        import jax, jax.numpy as jnp
        import numpy as np
        D = 256
        H = 16
        HD = D // H
        INNER = 4 * D
        EPS = 1e-05

        def layer_norm(x, w, b):
            mu = jnp.mean(x, axis=-1, keepdims=True)
            var = jnp.mean(jnp.square(x - mu), axis=-1, keepdims=True)
            return (x - mu) * jax.lax.rsqrt(var + EPS) * w + b
        key = jax.random.key(seed)
        ks = jax.random.split(key, 12)
        B, LQ, LK = (4, 128, 256)
        std = 0.02
        inp = {'hidden_states': jax.random.normal(ks[0], (B, LQ, D), jnp.float32), 'encoder_hidden_states': jax.random.normal(ks[1], (B, LK, D), jnp.float32), 'encoder_attention_mask': jnp.ones((B, LK), dtype=bool), 'ln1_w': jnp.ones((D,), jnp.float32), 'ln1_b': jnp.zeros((D,), jnp.float32), 'q_w': jax.random.normal(ks[2], (D, D), jnp.float32) * std, 'q_b': jnp.zeros((D,), jnp.float32), 'k_w': jax.random.normal(ks[3], (D, D), jnp.float32) * std, 'k_b': jnp.zeros((D,), jnp.float32), 'v_w': jax.random.normal(ks[4], (D, D), jnp.float32) * std, 'v_b': jnp.zeros((D,), jnp.float32), 'cproj_w': jax.random.normal(ks[5], (D, D), jnp.float32) * std, 'cproj_b': jnp.zeros((D,), jnp.float32), 'ln2_w': jnp.ones((D,), jnp.float32), 'ln2_b': jnp.zeros((D,), jnp.float32), 'fc_w': jax.random.normal(ks[6], (D, INNER), jnp.float32) * std, 'fc_b': jnp.zeros((INNER,), jnp.float32), 'proj_w': jax.random.normal(ks[7], (INNER, D), jnp.float32) * std, 'proj_b': jnp.zeros((D,), jnp.float32)}
        return inp
    _L0_xattn_all = _L0_xattn_setup()
    _L0_xattn_in = {k: v for k, v in _L0_xattn_all.items() if k in ('ln1_w', 'ln1_b', 'q_w', 'q_b', 'k_w', 'k_b', 'v_w', 'v_b', 'cproj_w', 'cproj_b', 'ln2_w', 'ln2_b', 'fc_w', 'fc_b', 'proj_w', 'proj_b')}
    del _L0_xattn_all
    return {'x': x, 'ctx_2048': ctx_2048, 'mask_BxS2_bf1': mask_BxS2_bf1, 'L0_xattn_ln1_w': _L0_xattn_in['ln1_w'], 'L0_xattn_ln1_b': _L0_xattn_in['ln1_b'], 'L0_xattn_q_w': _L0_xattn_in['q_w'], 'L0_xattn_q_b': _L0_xattn_in['q_b'], 'L0_xattn_k_w': _L0_xattn_in['k_w'], 'L0_xattn_k_b': _L0_xattn_in['k_b'], 'L0_xattn_v_w': _L0_xattn_in['v_w'], 'L0_xattn_v_b': _L0_xattn_in['v_b'], 'L0_xattn_cproj_w': _L0_xattn_in['cproj_w'], 'L0_xattn_cproj_b': _L0_xattn_in['cproj_b'], 'L0_xattn_ln2_w': _L0_xattn_in['ln2_w'], 'L0_xattn_ln2_b': _L0_xattn_in['ln2_b'], 'L0_xattn_fc_w': _L0_xattn_in['fc_w'], 'L0_xattn_fc_b': _L0_xattn_in['fc_b'], 'L0_xattn_proj_w': _L0_xattn_in['proj_w'], 'L0_xattn_proj_b': _L0_xattn_in['proj_b']}

def reference(x, ctx_2048, mask_BxS2_bf1, L0_xattn_ln1_w, L0_xattn_ln1_b, L0_xattn_q_w, L0_xattn_q_b, L0_xattn_k_w, L0_xattn_k_b, L0_xattn_v_w, L0_xattn_v_b, L0_xattn_cproj_w, L0_xattn_cproj_b, L0_xattn_ln2_w, L0_xattn_ln2_b, L0_xattn_fc_w, L0_xattn_fc_b, L0_xattn_proj_w, L0_xattn_proj_b):
    import jax
    import jax.numpy as jnp

    def _L0_xattn_ref(hidden_states, encoder_hidden_states, encoder_attention_mask, ln1_w, ln1_b, q_w, q_b, k_w, k_b, v_w, v_b, cproj_w, cproj_b, ln2_w, ln2_b, fc_w, fc_b, proj_w, proj_b):
        import jax, jax.numpy as jnp
        import numpy as np
        D = 256
        H = 16
        HD = D // H
        INNER = 4 * D
        EPS = 1e-05

        def layer_norm(x, w, b):
            mu = jnp.mean(x, axis=-1, keepdims=True)
            var = jnp.mean(jnp.square(x - mu), axis=-1, keepdims=True)
            return (x - mu) * jax.lax.rsqrt(var + EPS) * w + b
        B, LQ, _ = hidden_states.shape
        LK = encoder_hidden_states.shape[1]
        residual = hidden_states
        x = layer_norm(hidden_states, ln1_w, ln1_b)
        q = (x @ q_w + q_b).reshape(B, LQ, H, HD).transpose(0, 2, 1, 3)
        k = (encoder_hidden_states @ k_w + k_b).reshape(B, LK, H, HD).transpose(0, 2, 1, 3)
        v = (encoder_hidden_states @ v_w + v_b).reshape(B, LK, H, HD).transpose(0, 2, 1, 3)
        scale = 1.0 / np.sqrt(HD).astype(np.float32)
        scores = jnp.einsum('bhqd,bhkd->bhqk', q, k) * scale
        mask = encoder_attention_mask[:, None, None, :]
        mask_value = jnp.finfo(scores.dtype).min
        scores = jnp.where(mask, scores, mask_value)
        attn = jax.nn.softmax(scores, axis=-1)
        out = jnp.einsum('bhqk,bhkd->bhqd', attn, v)
        out = out.transpose(0, 2, 1, 3).reshape(B, LQ, D)
        out = out @ cproj_w + cproj_b
        hidden = out + residual
        residual = hidden
        y = layer_norm(hidden, ln2_w, ln2_b)
        y = jax.nn.gelu(y @ fc_w + fc_b, approximate=True)
        y = y @ proj_w + proj_b
        return residual + y
    x = _L0_xattn_ref(x, ctx_2048, mask_BxS2_bf1, L0_xattn_ln1_w, L0_xattn_ln1_b, L0_xattn_q_w, L0_xattn_q_b, L0_xattn_k_w, L0_xattn_k_b, L0_xattn_v_w, L0_xattn_v_b, L0_xattn_cproj_w, L0_xattn_cproj_b, L0_xattn_ln2_w, L0_xattn_ln2_b, L0_xattn_fc_w, L0_xattn_fc_b, L0_xattn_proj_w, L0_xattn_proj_b)
    return x

_drawn_inputs = setup_inputs


def setup_inputs(seed=0):
    import zlib

    import numpy as np

    out = dict(_drawn_inputs(seed))
    spreads = {'L0_xattn_ln1_w': (1.0, 0.6),
     'L0_xattn_ln1_b': (0.0, 0.8),
     'L0_xattn_q_b': (0.0, 0.8),
     'L0_xattn_k_b': (0.0, 0.8),
     'L0_xattn_v_b': (0.0, 0.1),
     'L0_xattn_cproj_b': (0.0, 0.1),
     'L0_xattn_ln2_w': (1.0, 0.6),
     'L0_xattn_ln2_b': (0.0, 0.735),
     'L0_xattn_fc_b': (0.0, 0.1),
     'L0_xattn_proj_b': (0.0, 0.1)}
    factors = {'L0_xattn_q_w': 8.0, 'L0_xattn_k_w': 8.0}
    for name, (base, spread) in spreads.items():
        noise = np.random.default_rng([zlib.crc32(name.encode()), seed]).standard_normal(out[name].shape)
        drawn = base * np.exp(spread * noise) if base else spread * noise
        out[name] = jnp.asarray(drawn.astype(out[name].dtype))
    for name, factor in factors.items():
        out[name] = (out[name] * factor).astype(out[name].dtype)
    return out
```

```python
from contextlib import ExitStack

import numpy as np

import concourse.bass as bass
from concourse import mybir

F32 = mybir.dt.float32
F32R = mybir.dt.float32r
BF16 = mybir.dt.bfloat16
U8 = mybir.dt.uint8
ALU = mybir.AluOpType
ACT = mybir.ActivationFunctionType
AX = mybir.AxisListType

P = 128
B, LQ, LK, D = 8, 256, 1601, 256
H, HD = 16, 16
INNER = 4 * D
KC = D // P
TOK = B * LQ // P
QT = LQ // P
KT = -(-LK // P)
KP = KT * P
TAIL = LK - (KT - 1) * P
HG = 4
SLOTS = H // HG
HM = P // HD
VW = HD + 1
NT = [3, 3, 3, 4]
CH = len(NT)
T0 = [sum(NT[:c]) for c in range(CH)]
NK = [min(LK, (T0[c] + NT[c]) * P) - T0[c] * P for c in range(CH)]
NKE = [n + n % 2 for n in NK]
NKM = max(NKE)
ROWS = 6 * HD
MASKROW, MAXROW = ROWS, ROWS + 1
KROWS = ROWS + 4
SCALE = 1.0 / float(np.sqrt(HD))
EPS = 1e-5
MASKED = 1e30
TG = 512
NTG = B * LQ // TG
TT = TG // P
NI = INNER // P
QG = HG * LQ
PBUF = 4
LAG = 2
MAXSTEPS = [1, 3, 5, 7]

class Section:
    pass


ALLKEYS = [[(0, q, k, min(401, LK - k))] for q in range(QT) for k in range(0, LK, 401)]


def build(nc, x, ctx_t, mask, w_kv, w_qc, fc, pj, cols, rows, ident, out):
    stack = ExitStack()
    with stack:
        def sb(name, shape, dt, where=stack):
            return where.enter_context(nc.sbuf_tensor(name, shape, dt))

        def sem(name):
            return stack.enter_context(nc.semaphore(name))

        k_scr = nc.dram_tensor("k_scr", [B, 2, 3, P, KP], BF16).ap()
        v_scr = nc.dram_tensor("v_scr", [B, SLOTS, P, KT * HG * VW], F32).ap()
        q_scr = nc.dram_tensor("q_scr", [2, 6, P, B * LQ], BF16).ap()
        mask_scr = nc.dram_tensor("mask_scr", [B, LK], BF16).ap()
        some_scr = nc.dram_tensor("some_scr", [1, B], F32).ap()

        S = stack.enter_context(nc.psum_tensor("S", [P, 4, 512], F32))
        O = stack.enter_context(nc.psum_tensor("O", [P, 2, 512], F32))
        MB = stack.enter_context(nc.psum_tensor("MB", [P, 512], F32))
        XB = stack.enter_context(nc.psum_tensor("XB", [P, 512], F32))

        idn = sb("idn", [P, P], F32)
        xs = sb("xs", [P, TOK, D], F32)
        hid = sb("hid", [P, TOK, D], F32)
        st = sb("st", [P, TOK, 6], F32)
        mv1 = sb("mv1", [P, TOK, 2], F32)
        mv2 = sb("mv2", [P, TOK, 2], F32)
        rs = sb("rs", [P, 4, TOK], F32)
        cols_s = sb("cols_s", [P, 20], F32)
        rows_s = sb("rows_s", [P, 3, D], F32)
        w_qc_s = sb("w_qc_s", [P, 2, KC, D], F32)
        some = sb("some", [P, B], F32)
        ln1_w, ln1_b, ln2_w, ln2_b = (cols_s[:, 2 * i:2 * i + 2] for i in range(4))
        bq_s, bk_s, fcb_s = cols_s[:, 8:10], cols_s[:, 10:12], cols_s[:, 12:20]
        bv_s, bc_s, pjb_s = (rows_s[:, i, :] for i in range(3))

        mid = ExitStack()
        kst = sb("kst", [P, SLOTS, HG, KP], BF16, mid)
        qst = sb("qst", [P, SLOTS, HG, LQ], BF16, mid)
        vsl = sb("vsl", [P, SLOTS, KT, HG * VW], F32, mid)

        early = ExitStack()
        w_raw = sb("w_raw", [P, 2, KC, D], F32, early)
        w_hi = sb("w_hi", [P, 2, KC, D], F32R, early)
        w_lo = sb("w_lo", [P, 2, KC, D], F32R, early)
        cT = sb("cT", [P, CH, KC, NKM], F32, early)
        c_hi = sb("c_hi", [P, 2, KC, NKM], F32R, early)
        c_lo = sb("c_lo", [P, 2, KC, NKM], F32R, early)
        kpart = sb("kpart", [P, 2, 2, 3, NKM], BF16, early)
        kres = sb("kres", [P, 2, NKM], F32, early)
        vst = sb("vst", [P, 2, SLOTS, max(NT), HG * VW], F32, early)
        ones = sb("ones", [3, KP], BF16, early)
        mk_u = sb("mk_u", [B, LK], U8, early)
        mk_f = sb("mk_f", [B, LK], F32, early)
        mk_b = sb("mk_b", [B, LK], BF16, early)
        some_b = sb("some_b", [B, 2], F32, early)
        qf = sb("qf", [P, 2, TG], F32, early)
        qres = sb("qres", [P, 2, TG], F32, early)
        qpart = sb("qpart", [P, 2, 3, TG], BF16, early)
        early.close()
        xn = hid[:, 0:8, :].rearrange("p (a t) d -> p a t d", a=2)
        xT = hid[:, 8:16, :].rearrange("p (a k u) d -> p a k (u d)", a=2, k=KC)

        late = ExitStack()
        fc_raw = sb("fc_raw", [P, KC, INNER], F32, late)
        pj_raw = sb("pj_raw", [P, NI, D], F32, late)
        fc_hi = sb("fc_hi", [P, KC, INNER], F32R, late)
        fc_lo = sb("fc_lo", [P, KC, INNER], F32R, late)
        pj_hi = sb("pj_hi", [P, NI, D], F32R, late)
        pj_lo = sb("pj_lo", [P, NI, D], F32R, late)
        pr = sb("pr", [P, PBUF, QG], F32, late)
        mxp = sb("mxp", [P, QT, HG, 4], F32, late)
        mx = sb("mx", [P, 2, QT, HG], F32, late)
        mres = sb("mres", [HG, LQ], F32, late)
        mrow = sb("mrow", [HG, 2, 3, LQ], BF16, late)
        osb = sb("osb", [P, 2, LQ], F32, late)
        rec = sb("rec", [P, QT, HG], F32, late)
        att = sb("att", [P, QT, D], F32, late)
        attT = sb("attT", [P, KC, LQ], F32, late)
        late.close()

        mid.close()
        last = ExitStack()
        yn = sb("yn", [P, 2, TT, D], F32, last)
        yT = sb("yT", [P, 2, KC, TG], F32, last)
        y_hi = sb("y_hi", [P, 2, KC, TG], F32R, last)
        y_lo = sb("y_lo", [P, 2, KC, TG], F32R, last)
        g = sb("g", [P, 2, TG], F32, last)
        g_hi = sb("g_hi", [P, NI, TG], F32R, last)
        g_lo = sb("g_lo", [P, NI, TG], F32R, last)
        ob = sb("ob", [P, 2, D], F32, last)
        last.close()

        cols_in, rows_in, wkv_in, wqc_in, idn_in, x_in, mask_in = map(
            sem, ("cols_in", "rows_in", "wkv_in", "wqc_in", "idn_in", "x_in", "mask_in"))
        ctx_in = [sem(f"ctx_in{c}") for c in range(CH)]
        k_out = [sem(f"k_out{i}") for i in range(2)]
        v_out = [sem(f"v_out{i}") for i in range(2)]
        q_out = [sem(f"q_out{i}") for i in range(2)]
        out_done = [sem(f"out_done{i}") for i in range(2)]
        mask_out, some_out, some_in, ones_in, mlpw_in = map(
            sem, ("mask_out", "some_out", "some_in", "ones_in", "mlpw_in"))
        pads_set, w_split, mask_steps = map(sem, ("pads_set", "w_split", "mask_steps"))
        hi_done, lo_done = sem("hi_done"), sem("lo_done")
        k_ready, kh_done, kres_done, km_done, kl_done = map(
            sem, ("k_ready", "kh_done", "kres_done", "km_done", "kl_done"))
        v_ready, v_done = sem("v_ready"), sem("v_done")
        st_steps, var_done, root_done, rstd_steps = map(sem, ("st_steps", "var_done", "root_done", "rstd_steps"))
        xn_done, xt_ready, xt_done, xb_done = map(sem, ("xn_done", "xt_ready", "xt_done", "xb_done"))
        q_ready, qf_done, qh_done, qres_done, qm_done, ql_done = map(
            sem, ("q_ready", "qf_done", "qh_done", "qres_done", "qm_done", "ql_done"))
        o_zeroed = sem("o_zeroed")
        mlpw_hi, mlpw_lo = sem("mlpw_hi"), sem("mlpw_lo")
        yn_done, yt_ready, yt_done, yhi_done, ylo_done = map(
            sem, ("yn_done", "yt_ready", "yt_done", "yhi_done", "ylo_done"))
        fc_ready, g_done, ghi_done, glo_done, pj_ready, ob_half, ob_done = map(
            sem, ("fc_ready", "g_done", "ghi_done", "glo_done", "pj_ready", "ob_half", "ob_done"))
        KRES0 = 4
        V0 = 4
        VR0 = NT[-1] + 1
        KL0 = OUT0 = 1
        EXP0 = 2
        O0 = 2

        def section(name, maxima):
            s = Section()
            s.maxima = maxima
            s.uses = HG * len(maxima) + 1
            s.slot_in = [sem(f"{name}_slot_in{i}") for i in range(SLOTS)]
            s.mrow_in = [sem(f"{name}_mrow_in{i}") for i in range(SLOTS)]
            s.scores_done = sem(f"{name}_scores_done")
            s.exp_done = sem(f"{name}_exp_done")
            s.o_ready = sem(f"{name}_o_ready")
            s.o_taken = sem(f"{name}_o_taken")
            s.max_ready = sem(f"{name}_max_ready")
            s.max_taken = sem(f"{name}_max_taken")
            s.mx_done = sem(f"{name}_mx_done")
            s.m_steps = sem(f"{name}_m_steps")
            s.mrow_done = sem(f"{name}_mrow_done")
            s.x_ready = sem(f"{name}_x_ready")
            s.x_taken = sem(f"{name}_x_taken")
            s.rec_done = sem(f"{name}_rec_done")
            s.h_steps = sem(f"{name}_h_steps")
            return s

        XU = SLOTS + 2
        sec = section("att", ALLKEYS)
        block = stack.enter_context(nc.Block())

        def v_bank(kt):
            return (O[:, 0, :], O[:, 1, :], MB[:, :], XB[:, :])[kt % 4]

        @block.sync
        def _(sp):
            def load_ctx(b, c):
                sp.dma_start(cT[:, c, :, 0:NK[c]], ctx_t[bass.ds(b, 1), :, :, T0[c] * P:T0[c] * P + NK[c]]
                             .rearrange("o k p t -> p (o k) t")).then_inc(ctx_in[c], 16)

            def store_kv(b, c):
                i, t, n = c % 2, T0[c] * P, NK[c]
                sp.wait_ge(kl_done, KL0 + 2 * (CH * b + c + 1))
                for mt in range(2):
                    sp.dma_start(k_scr[bass.ds(b, 1), mt, :, :, t:t + n].rearrange("o r p t -> p (o r) t"),
                                 kpart[:, i, mt, :, 0:n]).then_inc(k_out[i], 16)
                sp.wait_ge(v_done, V0 + KT * b + T0[c] + NT[c])
                sp.dma_start(v_scr[bass.ds(b, 1), :, :, T0[c] * HG * VW:(T0[c] + NT[c]) * HG * VW]
                             .rearrange("o s p w -> p (o s) w"),
                             vst[:, i, :, 0:NT[c], :].rearrange("p s t w -> p s (t w)")).then_inc(v_out[i], 16)

            for i in range(2):
                sp.sem_inc(k_out[i], OUT0)
                sp.sem_inc(v_out[i], OUT0)
            sp.dma_start(w_raw[:], w_kv).then_inc(wkv_in, 16)
            for c in range(CH):
                load_ctx(0, c)
            sp.dma_start(w_qc_s[:], w_qc).then_inc(wqc_in, 16)
            sp.wait_ge(mask_steps, 4)
            sp.dma_start(mask_scr, mk_b[:]).then_inc(mask_out, 16)
            sp.dma_start(some_scr.rearrange("o b -> b o"), some_b[:, 1:2]).then_inc(some_out, 16)
            sp.wait_ge(some_out, 16)
            sp.dma_start(some[:], some_scr[0].partition_broadcast(P)).then_inc(some_in, 16)
            sp.wait_ge(pads_set, 5)
            sp.dma_start(kst[MAXROW:MAXROW + 3, :, :, :].rearrange("p s h t -> p (s h) t"),
                         ones[:].unsqueeze(1).broadcast_to([3, H, KP])).then_inc(ones_in, 16)
            sp.dma_start(qst[MASKROW:MASKROW + 1, :, :, :].rearrange("p s h t -> p (s h) t"),
                         ones[0:1, 0:LQ].unsqueeze(1).broadcast_to([1, H, LQ])).then_inc(ones_in, 16)
            with sp.Fori(0, B - 1) as b:
                for c in range(CH):
                    sp.wait_ge(lo_done, CH * b + c + 1)
                    load_ctx(b + 1, c)
                    store_kv(b, c)
            for c in range(CH):
                store_kv(B - 1, c)

            def fill_kv(s_, b, s):
                rows_of = k_scr[bass.ds(b, 1), s // 2].rearrange("o r (d h) t -> (o r d) h t", h=HM)[
                    :, HG * (s % 2):HG * (s % 2) + HG, 0:LK]
                for r0, parts in ((0, 3), (3 * HD, 2), (5 * HD, 1)):
                    sp.dma_start(kst[r0:r0 + parts * HD, s, :, 0:LK], rows_of[0:parts * HD]
                                 ).then_inc(s_.slot_in[s], 16)
                sp.dma_start(kst[MASKROW:MASKROW + 1, s, :, 0:LK],
                             mask_scr[bass.ds(b, 1), :].unsqueeze(1).broadcast_to([1, HG, LK])
                             ).then_inc(s_.slot_in[s], 16)
                sp.dma_start(vsl[:, s, :, :].rearrange("p t w -> p (t w)"),
                             v_scr[bass.ds(b, 1), s].rearrange("o p w -> (o p) w")).then_inc(s_.slot_in[s], 16)

            def fill_q(s_, b, s):
                sp.dma_start(qst[0:ROWS, s, :, :], q_scr[s // 2].rearrange("g (d h) q -> (g d) h q", h=HM)[
                    :, HG * (s % 2):HG * (s % 2) + HG, bass.ds(b * LQ, LQ)]).then_inc(s_.slot_in[s], 16)

            for i in range(2):
                sp.wait_ge(k_out[i], OUT0 + 16 * 2 * B * CH // 2)
                sp.wait_ge(v_out[i], OUT0 + 16 * B * CH // 2)
            sp.wait_ge(mask_out, 16)
            sp.wait_ge(ones_in, 32)
            for s in range(SLOTS - 1):
                fill_kv(sec, 0, s)
            for j in range(2 * NTG):
                sp.wait_ge(ql_done, j + 1)
                dst = q_scr[j % 2, :, :, j // 2 * TG:(j // 2 + 1) * TG].rearrange("g p q -> p g q")
                for part, g0, ng in ((0, 0, 3), (1, 3, 2), (2, 5, 1)):
                    sp.dma_start(dst[:, g0:g0 + ng, :], qpart[:, j % 2, part:part + 1, :].broadcast_to([P, ng, TG])
                                 ).then_inc(q_out[j % 2], 16)
            for i in range(2):
                sp.wait_ge(q_out[i], 16 * 3 * NTG)
            for s in range(SLOTS - 1):
                fill_q(sec, 0, s)

            def send_rows(s_, b, s):
                sp.wait_ge(s_.mrow_done, SLOTS * b + s + 1)
                for part in range(3):
                    r = MAXROW + part
                    sp.dma_start(qst[r:r + 1, s, :, :], mrow[:, s % 2, part, :]).then_inc(s_.mrow_in[s], 16)

            def attention(s_, b, final):
                for s in range(SLOTS):
                    if s == 0 or not final:
                        sp.wait_ge(s_.o_ready, SLOTS * b + s)
                        fill_kv(s_, b if s == 0 else b + 1, (s + 3) % SLOTS)
                        fill_q(s_, b if s == 0 else b + 1, (s + 3) % SLOTS)
                    if s < 2 or not final:
                        send_rows(s_, b if s < 2 else b + 1, (s + 2) % SLOTS)

            send_rows(sec, 0, 0)
            send_rows(sec, 0, 1)
            attention(sec, 0, False)
            sp.dma_start(fc_raw[:], fc).then_inc(mlpw_in, 16)
            sp.dma_start(pj_raw[:], pj).then_inc(mlpw_in, 16)
            with sp.Fori(1, B - 1) as b:
                attention(sec, b, False)
            attention(sec, B - 1, True)

            for t in range(TOK):
                sp.wait_ge(ob_done, t + 1)
                sp.dma_start(out[t * P:(t + 1) * P, :], ob[:, t % 2, :]).then_inc(out_done[t % 2], 16)
            for i in range(2):
                sp.wait_ge(out_done[i], 16 * TOK // 2)

        @block.gpsimd
        def _(pool):
            nc.gpsimd.memset(ones[:], 1.0).then_inc(pads_set, 1)
            nc.gpsimd.memset(cT[:, CH - 1, :, NK[-1]:NKM], 0.0).then_inc(pads_set, 1)
            nc.gpsimd.memset(vst[:], 1.0).then_inc(pads_set, 1)
            pool.wait_ge(pads_set, 3)
            nc.gpsimd.memset(vst[64:P, 1, :, NT[-1] - 1, :], 0.0).then_inc(pads_set, 1)
            pool.wait_ge(pads_set, 4)
            nc.gpsimd.memset(kst[:, :, :, LK:KP], 0.0).then_inc(pads_set, 1)
            pool.wait_ge(pads_set, 5)
            nc.gpsimd.memset(vst[64:TAIL, 1, :, NT[-1] - 1, :], 1.0).then_inc(pads_set, 1)

            with pool.Fori(0, B) as b:
                for c in range(CH):
                    pool.wait_ge(hi_done, CH * b + c + 1)
                    i, n = c % 2, NKE[c]
                    nc.gpsimd.tensor_tensor(c_lo[:, i, :, 0:n], cT[:, c, :, 0:n], c_hi[:, i, :, 0:n].bitcast(F32),
                                            ALU.subtract).then_inc(lo_done, 1)
            pool.wait_ge(rows_in, 16)
            pool.wait_ge(xn_done, TOK)
            nc.gpsimd.tensor_tensor(xs[:], xs[:], bc_s.unsqueeze(1).broadcast_to([P, TOK, D]),
                                    ALU.add).then_inc(xb_done, 1)

            pool.wait_ge(mlpw_in, 32)
            nc.gpsimd.tensor_copy(fc_hi[:], fc_raw[:]).then_inc(mlpw_hi, 1)
            nc.gpsimd.tensor_copy(pj_hi[:], pj_raw[:]).then_inc(mlpw_hi, 1)
            pool.wait_ge(mlpw_hi, 2)
            nc.gpsimd.tensor_tensor(fc_lo[:], fc_raw[:], fc_hi[:].bitcast(F32), ALU.subtract).then_inc(mlpw_lo, 1)
            nc.gpsimd.tensor_tensor(pj_lo[:], pj_raw[:], pj_hi[:].bitcast(F32), ALU.subtract).then_inc(mlpw_lo, 1)
            for c in range(NTG):
                pool.wait_ge(yhi_done, c + 1)
                if c >= 2:
                    pool.wait_ge(fc_ready, NI * (c - 1))
                nc.gpsimd.tensor_tensor(y_lo[:, c % 2], yT[:, c % 2], y_hi[:, c % 2].bitcast(F32),
                                        ALU.subtract).then_inc(ylo_done, 1)

        @block.scalar
        def _(act):
            act.dma_start(mk_u[:], mask).then_inc(mask_in, 16)
            act.dma_start(cols_s[:], cols).then_inc(cols_in, 16)
            act.dma_start(rows_s[:], rows.partition_broadcast(P)).then_inc(rows_in, 16)
            for i in range(2):
                act.dma_start(xs[:, 8 * i:8 * i + 8, :], x[8 * i:8 * i + 8].rearrange("n p d -> p n d")
                              ).then_inc(x_in, 16)
            act.dma_start(idn[:], ident).then_inc(idn_in, 16)

            two_back = [T0[CH - 1] - KT, 0] + T0[1:CH - 1]

            def high(b, c):
                act.wait_ge(ctx_in[c], 16 * (b + 1))
                act.wait_ge(v_ready, VR0 + KT * b + two_back[c])
                nc.scalar.activation(c_hi[:, c % 2, :, 0:NKE[c]], cT[:, c, :, 0:NKE[c]], ACT.Copy
                                     ).then_inc(hi_done, 1)

            def k_parts(b, c):
                i, n = c % 2, NK[c]
                act.wait_ge(k_out[i], OUT0 + 16 * 2 * (2 * b + c // 2))
                for mt in range(2):
                    j = 2 * c + mt
                    act.wait_ge(k_ready, 2 * CH * b + j + 1)
                    nc.scalar.activation(kpart[:, i, mt, 0, 0:n], S[:, j % 4, 0:n], ACT.Identity,
                                         bias=bk_s[:, mt:mt + 1]).then_inc(kh_done, 1)
                for mt in range(2):
                    act.wait_ge(kres_done, KRES0 + 2 * (CH * b + c) + mt + 1)
                    nc.scalar.activation(kpart[:, i, mt, 1, 0:n], kres[:, mt, 0:n], ACT.Copy).then_inc(km_done, 1)

            act.wait_ge(cols_in, 16)
            act.wait_ge(pads_set, 6)
            high(0, 0)
            with act.Fori(0, B - 1) as b:
                for c in range(CH):
                    high(b if c + 1 < CH else b + 1, (c + 1) % CH)
                    k_parts(b, c)
            for c in range(CH):
                if c + 1 < CH:
                    high(B - 1, c + 1)
                k_parts(B - 1, c)

            act.wait_ge(var_done, 1)
            nc.scalar.activation(rs[:, 1, :], rs[:, 0, :], ACT.Sqrt).then_inc(root_done, 1)

            def x_t(t):
                for k in range(KC):
                    act.wait_ge(xt_ready, KC * t + k + 1)
                    if t >= 2:
                        act.wait_ge(q_ready, 2 * (t - 1))
                    nc.scalar.activation(xT[:, t % 2, k, :], S[:, k, :], ACT.Identity,
                                         bias=ln1_b[:, k:k + 1], scale=ln1_w[:, k:k + 1]).then_inc(xt_done, 1)

            def q_parts(j):
                if j >= 2:
                    act.wait_ge(q_out[j % 2], 16 * 3 * (j // 2))
                act.wait_ge(qf_done, j + 1)
                nc.scalar.activation(qpart[:, j % 2, 0, :], qf[:, j % 2, :], ACT.Copy).then_inc(qh_done, 1)
                act.wait_ge(qres_done, j + 1)
                nc.scalar.activation(qpart[:, j % 2, 1, :], qres[:, j % 2, :], ACT.Copy).then_inc(qm_done, 1)

            for t in range(NTG + 1):
                if t < NTG:
                    x_t(t)
                if t >= 1:
                    q_parts(2 * (t - 1))
                    q_parts(2 * (t - 1) + 1)

            assert PBUF >= LAG + 2 and (SLOTS * KT) % PBUF == 0 and (SLOTS * KT) % 2 == 0

            def attention(s_, b):
                for n in range(SLOTS * KT):
                    act.wait_ge(s_.scores_done, SLOTS * KT * b + n + 1)
                    nc.scalar.activation(pr[:, n % PBUF, :], S[:, 2 * (n % 2):2 * (n % 2) + 2, :]
                                         .rearrange("p a n -> p (a n)"), ACT.Exp).then_inc(s_.exp_done, 1)

            act.sem_inc(sec.exp_done, EXP0)
            with act.Fori(0, B) as b:
                attention(sec, b)

            act.wait_ge(var_done, 2)
            nc.scalar.activation(rs[:, 1, :], rs[:, 0, :], ACT.Sqrt).then_inc(root_done, 1)

            def y_t(c):
                for k in range(KC):
                    act.wait_ge(yt_ready, KC * c + k + 1)
                    if c >= 2:
                        act.wait_ge(ylo_done, c - 1)
                    nc.scalar.activation(yT[:, c % 2, k, :], (MB, XB)[k][:, :], ACT.Identity,
                                         bias=ln2_b[:, k:k + 1], scale=ln2_w[:, k:k + 1]).then_inc(yt_done, 1)

            y_t(0)
            for c in range(NTG):
                for i in range(NI):
                    j = NI * c + i
                    act.wait_ge(fc_ready, j + 1)
                    if j >= 2:
                        act.wait_ge(glo_done, j - 1)
                    nc.scalar.activation(g[:, j % 2, :], S[:, j % 4, :], ACT.Gelu_apprx_tanh,
                                         bias=fcb_s[:, i:i + 1]).then_inc(g_done, 1)
                    if i == 4 and c + 1 < NTG:
                        y_t(c + 1)

        @block.vector
        def _(dve):
            dve.sem_inc(kres_done, KRES0)
            dve.sem_inc(kl_done, KL0)
            dve.sem_inc(v_done, V0)
            dve.sem_inc(sec.o_taken, O0)
            dve.wait_ge(wkv_in, 16)
            nc.vector.tensor_copy(w_hi[:], w_raw[:]).then_inc(w_split, 1)
            dve.wait_ge(w_split, 1)
            nc.vector.tensor_tensor(w_lo[:], w_raw[:], w_hi[:].bitcast(F32), ALU.subtract).then_inc(w_split, 1)
            dve.wait_ge(mask_in, 16)
            nc.vector.tensor_copy(mk_f[:], mk_u[:]).then_inc(mask_steps, 1)
            dve.wait_ge(mask_steps, 1)
            nc.vector.tensor_reduce(some_b[:, 0:1], mk_f[:], AX.X, ALU.max).then_inc(mask_steps, 1)
            dve.wait_ge(mask_steps, 2)
            nc.vector.tensor_scalar(mk_b[:], mk_f[:], some_b[:, 0:1], MASKED, ALU.subtract, ALU.mult
                                    ).then_inc(mask_steps, 1)
            nc.vector.tensor_scalar(some_b[:, 1:2], some_b[:, 0:1], SCALE, None, ALU.mult).then_inc(mask_steps, 1)

            def k_rest(b, c):
                i, n = c % 2, NK[c]
                dve.wait_ge(kl_done, KL0 + 2 * (CH * b + c))
                for mt in range(2):
                    j = 2 * c + mt
                    dve.wait_ge(kh_done, 2 * CH * b + j + 1)
                    nc.vector.scalar_tensor_tensor(out=kres[:, mt, 0:n], in0=S[:, j % 4, 0:n],
                                                   scalar=bk_s[:, mt:mt + 1], in1=kpart[:, i, mt, 0, 0:n],
                                                   op0=ALU.add, op1=ALU.subtract).then_inc(kres_done, 1)

            def k_low(b, c):
                i, n = c % 2, NK[c]
                for mt in range(2):
                    dve.wait_ge(km_done, 2 * (CH * b + c) + mt + 1)
                    nc.vector.tensor_tensor(kpart[:, i, mt, 2, 0:n], kres[:, mt, 0:n], kpart[:, i, mt, 1, 0:n],
                                            ALU.subtract).then_inc(kl_done, 1)

            def v_tiles(b, c):
                dve.wait_ge(v_out[c % 2], OUT0 + 16 * (2 * b + c // 2))
                for t in range(NT[c]):
                    kt = T0[c] + t
                    m = TAIL if kt == KT - 1 else P
                    dve.wait_ge(v_ready, VR0 + KT * b + kt + 1)
                    nc.vector.tensor_tensor(
                        vst[0:m, c % 2, :, t, :].rearrange("p s (h w) -> p s h w", w=VW)[:, :, :, 0:HD],
                        v_bank(kt)[0:m, 0:D].rearrange("p (s h d) -> p s h d", s=SLOTS, d=HD),
                        bv_s[0:m, :].rearrange("p (s h d) -> p s h d", s=SLOTS, d=HD), ALU.add).then_inc(v_done, 1)

            dve.wait_ge(cols_in, 16)
            dve.wait_ge(rows_in, 16)
            dve.wait_ge(x_in, 32)
            dve.wait_ge(pads_set, 6)
            with dve.Fori(0, B) as b:
                for c in range(CH):
                    k_rest(b, c)
                    k_low(b, c)
                    v_tiles(b, c)
                for q in range(QT):
                    nc.vector.bn_stats(st[:, bass.ds(QT * b + q, 1), :], xs[:, bass.ds(QT * b + q, 1), :]
                                       ).then_inc(st_steps, 1)

            def moments(mv, tiles):
                for n in tiles:
                    nc.vector.bn_aggr(mv[:, n, :], st[:, n, :]).then_inc(rstd_steps, 1)

            def rstd(mv, before, run):
                dve.wait_ge(rstd_steps, before)
                nc.vector.tensor_scalar(rs[:, 0, :], mv[:, :, 1], EPS, None, ALU.add).then_inc(var_done, 1)
                dve.wait_ge(root_done, run)
                nc.vector.reciprocal(rs[:, 2, :], rs[:, 1, :]).then_inc(rstd_steps, 1)
                dve.wait_ge(rstd_steps, before + 1)
                nc.vector.tensor_tensor(rs[:, 3, :], rs[:, 0, :], rs[:, 2, :], ALU.mult).then_inc(rstd_steps, 1)
                dve.wait_ge(rstd_steps, before + 2)
                nc.vector.tensor_tensor(rs[:, 3, :], rs[:, 3, :], rs[:, 2, :], ALU.mult).then_inc(rstd_steps, 1)
                dve.wait_ge(rstd_steps, before + 3)
                nc.vector.tensor_scalar(rs[:, 3, :], rs[:, 3, :], -0.5, 1.5, ALU.mult, ALU.add
                                        ).then_inc(rstd_steps, 1)
                dve.wait_ge(rstd_steps, before + 4)
                nc.vector.tensor_tensor(rs[:, 2, :], rs[:, 2, :], rs[:, 3, :], ALU.mult).then_inc(rstd_steps, 1)
                dve.wait_ge(rstd_steps, before + 5)

            def normalise(dst, src, mv, t, done, read):
                if t >= 2:
                    dve.wait_ge(read, KC * (t - 1))
                for i in range(TT):
                    n = TT * t + i
                    nc.vector.tensor_scalar(dst[:, t % 2, i, :], src[:, n, :], mv[:, n, 0:1], rs[:, 2, n:n + 1],
                                            ALU.subtract, ALU.mult).then_inc(done, 1)

            def q_rest(j):
                i, t = j % 2, j // 2
                dve.wait_ge(q_ready, j + 1)
                for half in range(TG // LQ):
                    b = TG // LQ * t + half
                    last = nc.vector.tensor_scalar(
                        qf[:, i, half * LQ:(half + 1) * LQ], S[:, 2 + i, half * LQ:(half + 1) * LQ],
                        bq_s[:, i:i + 1], some[:, b:b + 1], ALU.add, ALU.mult)
                last.then_inc(qf_done, 1)
                dve.wait_ge(qh_done, j + 1)
                nc.vector.tensor_tensor(qres[:, i, :], qf[:, i, :], qpart[:, i, 0, :], ALU.subtract
                                        ).then_inc(qres_done, 1)
                dve.wait_ge(qm_done, j + 1)
                nc.vector.tensor_tensor(qpart[:, i, 2, :], qres[:, i, :], qpart[:, i, 1, :], ALU.subtract
                                        ).then_inc(ql_done, 1)

            dve.wait_ge(st_steps, TOK)
            moments(mv1, range(TOK))
            rstd(mv1, TOK, 1)
            dve.wait_ge(some_in, 16)
            normalise(xn, xs, mv1, 0, xn_done, xt_ready)
            for t in range(NTG):
                if t + 1 < NTG:
                    normalise(xn, xs, mv1, t + 1, xn_done, xt_ready)
                q_rest(2 * t)
                q_rest(2 * t + 1)

            nc.vector.memset(O[:, :, 0:LQ], 0.0).then_inc(o_zeroed, 1)

            def maxima_of(s_, n, s, h):
                for i, products in enumerate(s_.maxima):
                    use = s_.uses * n + h * len(s_.maxima) + i
                    dve.wait_ge(s_.max_ready, use + 1)
                    _, q, k, w = products[0]
                    nc.vector.tensor_reduce(mxp[:, q, h, i % 4:i % 4 + 1], MB[:, 0:w], AX.X, ALU.max
                                            ).then_inc(s_.max_taken, 1)
                if h == HG - 1:
                    dve.wait_ge(s_.max_taken, s_.uses * n + HG * len(s_.maxima))
                    nc.vector.tensor_reduce(mx[:, s % 2], mxp[:], AX.X, ALU.max, negate=True
                                            ).then_inc(s_.mx_done, 1)

            def max_rows(s_, n, b, s):
                dve.wait_ge(s_.max_ready, s_.uses * (n + 1))
                dve.wait_ge(s_.mrow_in[(s + 2) % SLOTS], 16 * 3 * (b if s < 2 else b + 1))
                hi, mi, lo = (mrow[:, s % 2, part, :] for part in range(3))
                nc.vector.tensor_copy(hi, MB[0:HG, 0:LQ]).then_inc(s_.m_steps, 1)
                dve.wait_ge(s_.m_steps, 2 * n + 1)
                nc.vector.tensor_tensor(mres[:], MB[0:HG, 0:LQ], hi, ALU.subtract).then_inc(s_.max_taken, 1)
                dve.wait_ge(s_.max_taken, s_.uses * (n + 1))
                nc.vector.tensor_copy(mi, mres[:]).then_inc(s_.m_steps, 1)
                dve.wait_ge(s_.m_steps, 2 * n + 2)
                nc.vector.tensor_tensor(lo, mres[:], mi, ALU.subtract).then_inc(s_.mrow_done, 1)

            def take_o(s_, n, s):
                dve.wait_ge(s_.o_ready, n + 1)
                nc.vector.tensor_copy(osb[:, s % 2, :], O[:, s % 2, 0:LQ]).then_inc(s_.o_taken, 1)

            def divide(s_, b, n, s):
                dve.wait_ge(s_.x_ready, XU * b + s + 1)
                ot = XB[:, 0:QT * P].rearrange("p (q h w) -> p q h w", q=QT, w=32)
                nc.vector.reciprocal(rec[:], ot[:, :, :, HD]).then_inc(s_.rec_done, 1)
                dve.wait_ge(s_.rec_done, n + 1)
                nc.vector.tensor_tensor(
                    att[:, :, s * HG * HD:(s + 1) * HG * HD].rearrange("p q (h d) -> p q h d", d=HD),
                    ot[:, :, :, 0:HD], rec[:].unsqueeze(3).broadcast_to([P, QT, HG, HD]), ALU.mult
                ).then_inc(s_.x_taken, 1)

            def take_att_t(s_, b):
                dve.wait_ge(s_.x_ready, XU * b + SLOTS + 1)
                nc.vector.tensor_copy(attT[:].rearrange("p k q -> p (k q)"), XB[:, :]).then_inc(s_.x_taken, 1)

            def hidden(s_, b):
                dve.wait_ge(s_.x_ready, XU * b + SLOTS + 2)
                rows_ = bass.ds(QT * b, QT)
                nc.vector.tensor_tensor(hid[:, rows_, :], XB[:, :].rearrange("p (q d) -> p q d", q=QT),
                                        xs[:, rows_, :], ALU.add).then_inc(s_.x_taken, 1)
                dve.wait_ge(s_.x_taken, XU * (b + 1))
                for q in range(QT):
                    last = nc.vector.bn_stats(st[:, bass.ds(QT * b + q, 1), :], hid[:, bass.ds(QT * b + q, 1), :])
                last.then_inc(s_.h_steps, 1)

            def attention(s_, b, first, final):
                for s in range(SLOTS):
                    n = SLOTS * b + s
                    b2 = b if s < 2 else b + 1
                    s2 = (s + 2) % SLOTS
                    before = not (first and s == 0)
                    ahead = s < 2 or not final
                    if ahead:
                        maxima_of(s_, n + 2, s2, 0)
                    if before:
                        take_o(s_, n - 1, (s - 1) % SLOTS)
                    if ahead:
                        maxima_of(s_, n + 2, s2, 1)
                    if before:
                        divide(s_, b if s else b - 1, n - 1, (s - 1) % SLOTS)
                    if ahead:
                        maxima_of(s_, n + 2, s2, 2)
                        maxima_of(s_, n + 2, s2, 3)
                    if before and s == 0:
                        take_att_t(s_, b - 1)
                    if ahead:
                        max_rows(s_, n + 2, b2, s2)
                    if before and s == 0:
                        hidden(s_, b - 1)

            def finish(s_, b):
                take_o(s_, SLOTS * (b + 1) - 1, SLOTS - 1)
                divide(s_, b, SLOTS * (b + 1) - 1, SLOTS - 1)
                take_att_t(s_, b)
                hidden(s_, b)

            for s in range(2):
                for h in range(HG):
                    maxima_of(sec, s, s, h)
                max_rows(sec, s, 0, s)
            dve.wait_ge(xb_done, 1)
            attention(sec, 0, True, False)
            with dve.Fori(1, B - 1) as b:
                attention(sec, b, False, False)
            attention(sec, B - 1, False, True)
            finish(sec, B - 1)

            dve.wait_ge(sec.h_steps, B)
            moments(mv2, range(TOK))
            rstd(mv2, 2 * TOK + 5, 2)
            normalise(yn, hid, mv2, 0, yn_done, yt_ready)

            def y_high(c):
                dve.wait_ge(yt_done, KC * (c + 1))
                if c >= 2:
                    dve.wait_ge(fc_ready, NI * (c - 1))
                nc.vector.tensor_copy(y_hi[:, c % 2], yT[:, c % 2]).then_inc(yhi_done, 1)

            y_high(0)
            for c in range(NTG):
                for i in range(NI):
                    j = NI * c + i
                    dve.wait_ge(g_done, j + 1)
                    nc.vector.tensor_copy(g_hi[:, i, :], g[:, j % 2, :]).then_inc(ghi_done, 1)
                    dve.wait_ge(ghi_done, j + 1)
                    nc.vector.tensor_tensor(g_lo[:, i, :], g[:, j % 2, :], g_hi[:, i, :].bitcast(F32), ALU.subtract
                                            ).then_inc(glo_done, 1)
                    if i == 1 and c + 1 < NTG:
                        normalise(yn, hid, mv2, c + 1, yn_done, yt_ready)
                    if i == 6 and c + 1 < NTG:
                        y_high(c + 1)
                for t in range(TT):
                    n = TT * c + t
                    dve.wait_ge(pj_ready, n + 1)
                    if n >= 2:
                        dve.wait_ge(out_done[n % 2], 16 * (n // 2))
                    nc.vector.tensor_tensor(ob[:, n % 2, :], O[:, n % 2, 0:D], pjb_s, ALU.add).then_inc(ob_half, 1)
                    dve.wait_ge(ob_half, n + 1)
                    nc.vector.tensor_tensor(ob[:, n % 2, :], ob[:, n % 2, :], hid[:, n, :], ALU.add
                                            ).then_inc(ob_done, 1)

        @block.tensor
        def _(pe):
            def product3(dst, w, m):
                terms = [(a, c) for (wh, wl), (mh, ml) in zip(w, m) for a, c in ((wh, mh), (wh, ml), (wl, mh))]
                for i, (a, c) in enumerate(terms):
                    last = nc.tensor.matmul(dst, a, c, start=i == 0, stop=i == len(terms) - 1)
                return last

            pe.sem_inc(v_ready, VR0)
            pe.wait_ge(w_split, 2)
            with pe.Fori(0, B) as b:
                for c in range(CH):
                    i, n = c % 2, NKE[c]
                    pe.wait_ge(lo_done, CH * b + c + 1)
                    for mt in range(2):
                        j = 2 * c + mt
                        pe.wait_ge(kres_done, 2 * CH * b + j + 1)
                        cut = slice(mt * P, (mt + 1) * P)
                        product3(S[:, j % 4, 0:n], [(w_hi[:, 0, k, cut], w_lo[:, 0, k, cut]) for k in range(KC)],
                                 [(c_hi[:, i, k, 0:n], c_lo[:, i, k, 0:n]) for k in range(KC)]
                                 ).then_inc(k_ready, 1)
                    for t in range(NT[c]):
                        kt = T0[c] + t
                        m = TAIL if kt == KT - 1 else P
                        pe.wait_ge(v_done, KT * b + (V0 if kt == 0 else kt if kt < 4 else kt + 1))
                        cut = slice(t * P, t * P + m)
                        product3(v_bank(kt)[0:m, 0:D], [(c_hi[:, i, k, cut], c_lo[:, i, k, cut]) for k in range(KC)],
                                 [(w_hi[:, 1, k, :], w_lo[:, 1, k, :]) for k in range(KC)]).then_inc(v_ready, 1)

            pe.wait_ge(idn_in, 16)
            pe.wait_ge(wqc_in, 16)
            pe.wait_ge(kres_done, KRES0 + 2 * CH * B)

            def turn(dst, src, t, normed, taken, ready):
                for i in range(TT):
                    pe.wait_ge(normed, TT * t + i + 1)
                    for k in range(KC):
                        if t >= 1 and i == 0:
                            pe.wait_ge(taken, KC * (t - 1) + k + 1)
                        last = nc.tensor.transpose(dst[k][:, i * P:(i + 1) * P],
                                                   src[:, t % 2, i, k * P:(k + 1) * P], idn[:])
                        if i == TT - 1:
                            last.then_inc(ready, 1)

            def q_product(t):
                for mt in range(2):
                    j = 2 * t + mt
                    pe.wait_ge(xt_done, KC * (t + 1))
                    if j >= 2:
                        pe.wait_ge(qf_done, j - 1)
                    for k in range(KC):
                        last = nc.tensor.matmul(S[:, 2 + mt, :], w_qc_s[:, 0, k, mt * P:(mt + 1) * P],
                                                xT[:, t % 2, k, :], start=k == 0, stop=k == KC - 1)
                    last.then_inc(q_ready, 1)

            turn((S[:, 0, :], S[:, 1, :]), xn, 0, xn_done, xt_done, xt_ready)
            for t in range(NTG):
                if t + 1 < NTG:
                    turn((S[:, 0, :], S[:, 1, :]), xn, t + 1, xn_done, xt_done, xt_ready)
                q_product(t)

            def maxima_of(s_, n, b, s, h):
                if h == 0:
                    pe.wait_ge(s_.slot_in[s], 16 * 6 * (b + 1))
                for i, products in enumerate(s_.maxima):
                    pe.wait_ge(s_.max_taken, s_.uses * n + h * len(s_.maxima) + i)
                    for col, q, k, w in products:
                        last = nc.tensor.matmul(MB[:, col:col + w], qst[0:MASKROW + 1, s, h, q * P:(q + 1) * P],
                                                kst[0:MASKROW + 1, s, h, k:k + w], start=True, stop=True)
                    last.then_inc(s_.max_ready, 1)

            def max_rows(s_, n, s):
                pe.wait_ge(s_.max_taken, s_.uses * (n + 1) - 1)
                pe.wait_ge(s_.mx_done, n + 1)
                for q in range(QT):
                    last = nc.tensor.matmul(MB[0:HG, q * P:(q + 1) * P], mx[:, s % 2, q, :], idn[:],
                                            start=True, stop=True)
                last.then_inc(s_.max_ready, 1)

            def scores(s_, b, s, kt):
                n = s * KT + kt
                if kt == 0:
                    pe.wait_ge(s_.mrow_in[s], 16 * 3 * (b + 1))
                pe.wait_ge(s_.exp_done, SLOTS * KT * b + n + 1)
                for h in range(HG):
                    last = nc.tensor.matmul(S[:, 2 * (n % 2) + h // 2, (h % 2) * LQ:(h % 2 + 1) * LQ],
                                            kst[0:KROWS, s, h, kt * P:(kt + 1) * P], qst[0:KROWS, s, h, :],
                                            start=True, stop=True)
                last.then_inc(s_.scores_done, 1)

            def values(s_, b, s, kt):
                if kt == 0:
                    pe.wait_ge(s_.o_taken, SLOTS * b + s + 1)
                for h in range(HG):
                    last = nc.tensor.matmul(O[32 * h:32 * h + VW, s % 2, 0:LQ], vsl[:, s, kt, h * VW:(h + 1) * VW],
                                            pr[:, (s * KT + kt) % PBUF, h * LQ:(h + 1) * LQ],
                                            start=kt == 0, stop=kt == KT - 1, skip_group_check=True)
                if kt == KT - 1:
                    last.then_inc(s_.o_ready, 1)

            def turn_o(s_, b, n, s):
                pe.wait_ge(s_.o_taken, O0 + n + 1)
                pe.wait_ge(s_.x_taken, XU * b + s)
                for q in range(QT):
                    last = nc.tensor.transpose(XB[:, q * P:(q + 1) * P], osb[:, s % 2, q * P:(q + 1) * P], idn[:])
                last.then_inc(s_.x_ready, 1)

            def turn_att(s_, b):
                pe.wait_ge(s_.x_taken, XU * b + SLOTS)
                for k in range(KC):
                    for q in range(QT):
                        last = nc.tensor.transpose(XB[:, k * LQ + q * P:k * LQ + (q + 1) * P],
                                                   att[:, q, k * P:(k + 1) * P], idn[:])
                last.then_inc(s_.x_ready, 1)

            def project(s_, b):
                pe.wait_ge(s_.x_taken, XU * b + SLOTS + 1)
                for q in range(QT):
                    for k in range(KC):
                        last = nc.tensor.matmul(XB[:, q * D:(q + 1) * D], attT[:, k, q * P:(q + 1) * P],
                                                w_qc_s[:, 1, k, :], start=k == 0, stop=k == KC - 1)
                last.then_inc(s_.x_ready, 1)

            def attention(s_, b, first, final):
                for s in range(SLOTS):
                    n = SLOTS * b + s
                    b2 = b if s < 2 else b + 1
                    s2 = (s + 2) % SLOTS
                    before = not (first and s == 0)
                    ahead = s < 2 or not final
                    for kt in range(KT):
                        scores(s_, b, s, kt)
                        if ahead and kt in MAXSTEPS:
                            maxima_of(s_, n + 2, b2, s2, MAXSTEPS.index(kt))
                        if before and kt == 4:
                            turn_o(s_, b if s else b - 1, n - 1, (s - 1) % SLOTS)
                        if before and s == 0 and kt == 8:
                            turn_att(s_, b - 1)
                        if ahead and kt == 9:
                            max_rows(s_, n + 2, s2)
                        if before and s == 0 and kt == 11:
                            project(s_, b - 1)
                        if kt >= LAG:
                            values(s_, b, s, kt - LAG)
                        elif before:
                            values(s_, b if s else b - 1, (s - 1) % SLOTS, KT + kt - LAG)

            def finish(s_, b):
                for kt in range(KT - LAG, KT):
                    pe.wait_ge(s_.exp_done, EXP0 + SLOTS * KT * (b + 1) - KT + kt + 1)
                    values(s_, b, SLOTS - 1, kt)
                turn_o(s_, b, SLOTS * (b + 1) - 1, SLOTS - 1)
                turn_att(s_, b)
                project(s_, b)

            pe.wait_ge(qf_done, 2 * NTG)
            pe.wait_ge(xt_done, KC * NTG)
            pe.wait_ge(v_done, V0 + KT * B)
            for s in range(2):
                for h in range(HG):
                    maxima_of(sec, s, 0, s, h)
                max_rows(sec, s, s)
            pe.wait_ge(o_zeroed, 1)
            attention(sec, 0, True, False)
            with pe.Fori(1, B - 1) as b:
                attention(sec, b, False, False)
            attention(sec, B - 1, False, True)
            finish(sec, B - 1)

            pe.wait_ge(mlpw_lo, 2)
            pe.wait_ge(sec.max_taken, sec.uses * SLOTS * B)
            pe.wait_ge(sec.x_taken, XU * B)
            turn((MB[:, :], XB[:, :]), yn, 0, yn_done, yt_done, yt_ready)
            for c in range(NTG):
                pe.wait_ge(ylo_done, c + 1)
                for i in range(NI):
                    j = NI * c + i
                    if j >= 4:
                        pe.wait_ge(g_done, j - 3)
                    cut = slice(i * P, (i + 1) * P)
                    product3(S[:, j % 4, :], [(fc_hi[:, k, cut], fc_lo[:, k, cut]) for k in range(KC)],
                             [(y_hi[:, c % 2, k, :], y_lo[:, c % 2, k, :]) for k in range(KC)]).then_inc(fc_ready, 1)
                    if i == 3 and c + 1 < NTG:
                        turn((MB[:, :], XB[:, :]), yn, c + 1, yn_done, yt_done, yt_ready)
                for t in range(TT):
                    n = TT * c + t
                    if n >= 2:
                        pe.wait_ge(ob_half, n - 1)
                    for i in range(NI):
                        if t == 0:
                            pe.wait_ge(glo_done, NI * c + i + 1)
                        cut = slice(t * P, (t + 1) * P)
                        for m, (w, v) in enumerate(((g_hi, pj_hi), (g_hi, pj_lo), (g_lo, pj_hi))):
                            last = nc.tensor.matmul(O[:, n % 2, 0:D], w[:, i, cut], v[:, i, :],
                                                    start=i == 0 and m == 0, stop=i == NI - 1 and m == 2)
                    last.then_inc(pj_ready, 1)


def kernel(x, ctx_2048, mask_BxS2_bf1, **w):
    import concourse.bacc as bacc
    from concourse.bass_utils import run_bass_kernel_spmd

    w = {n.removeprefix("L0_xattn_"): np.asarray(a) for n, a in w.items()}
    con = np.ascontiguousarray

    def chunks(a):
        return a.reshape(-1, P, a.shape[-1]).transpose(1, 0, 2)

    def by_width(a):
        return a.reshape(*a.shape[:-1], 2, HM, HD).swapaxes(-1, -2).reshape(a.shape)

    def column(a):
        return a.reshape(-1, P).T

    arrays = {
        "x": con(np.asarray(x).reshape(TOK, P, D)),
        "ctx_t": con(np.asarray(ctx_2048).transpose(0, 2, 1).reshape(B, KC, P, LK)),
        "mask": con(np.asarray(mask_BxS2_bf1)).view(np.uint8),
        "w_kv": con(np.stack([chunks(by_width(w["k_w"])), chunks(w["v_w"])], 1)),
        "w_qc": con(np.stack([chunks(by_width(w["q_w"])), chunks(w["cproj_w"])], 1)),
        "fc": con(chunks(w["fc_w"])),
        "pj": con(chunks(w["proj_w"])),
        "cols": con(np.concatenate([column(a) for a in (
            w["ln1_w"], w["ln1_b"], w["ln2_w"], w["ln2_b"], by_width(w["q_b"]), by_width(w["k_b"]), w["fc_b"])], 1)),
        "rows": con(np.stack([w["v_b"], w["cproj_b"], w["proj_b"]])),
        "ident": np.eye(P, dtype=np.float32),
    }
    nc = bacc.Bacc("TRN2", target_bir_lowering=False, num_devices=1)
    aps = {n: nc.dram_tensor(f"in_{n}", a.shape, mybir.dt.from_np(a.dtype), kind="ExternalInput").ap()
           for n, a in arrays.items()}
    out = nc.dram_tensor("out", [B * LQ, D], F32, kind="ExternalOutput").ap()
    build(nc, out=out, **aps)
    r = run_bass_kernel_spmd(nc, [{f"in_{n}": a for n, a in arrays.items()}], core_ids=[0])
    return r.results[0]["out"].reshape(B, LQ, D)
```

```python
from contextlib import ExitStack

import numpy as np

import concourse.bass as bass
from concourse import mybir

F32 = mybir.dt.float32
F32R = mybir.dt.float32r
BF16 = mybir.dt.bfloat16
U8 = mybir.dt.uint8
I32 = mybir.dt.int32
ALU = mybir.AluOpType
ACT = mybir.ActivationFunctionType
AX = mybir.AxisListType

P = 128
B, LQ, LK, D = 8, 256, 1601, 256
H, HD = 16, 16
INNER = 4 * D
KC = D // P
TOK = B * LQ // P
QT = LQ // P
KT = -(-LK // P)
KP = KT * P
TAIL = LK - (KT - 1) * P
HG = 4
SLOTS = H // HG
HM = P // HD
VW = HD + 1
NT = [3, 3, 3, 4]
CH = len(NT)
T0 = [sum(NT[:c]) for c in range(CH)]
NK = [min(LK, (T0[c] + NT[c]) * P) - T0[c] * P for c in range(CH)]
NKE = [n + n % 2 for n in NK]
NKM = max(NKE)
ROWS = 6 * HD
MASKROW, MAXROW = ROWS, ROWS + 1
KROWS = ROWS + 4
SCALE = 1.0 / float(np.sqrt(HD))
EPS = 1e-5
MASKED = 1e30
LARGE = 1e30
TG = 512
NTG = B * LQ // TG
TT = TG // P
NI = INNER // P
QG = HG * LQ
PBUF = 4
LAG = 2
MAXSTEPS = [1, 3, 5, 7]

class Section:
    pass


BLOCKKEYS = [[(q * 256, q, 0, 256) for q in range(QT)]]
ALLKEYS = [[(0, q, k, min(401, LK - k))] for q in range(QT) for k in range(0, LK, 401)]


def build(nc, x, ctx_t, mask, w_kv, w_qc, fc, pj, cols, rows, ident, out):
    stack = ExitStack()
    with stack:
        def sb(name, shape, dt, where=stack):
            return where.enter_context(nc.sbuf_tensor(name, shape, dt))

        def sem(name):
            return stack.enter_context(nc.semaphore(name))

        k_scr = nc.dram_tensor("k_scr", [B, 2, 3, P, KP], BF16).ap()
        v_scr = nc.dram_tensor("v_scr", [B, SLOTS, P, KT * HG * VW], F32).ap()
        q_scr = nc.dram_tensor("q_scr", [2, 6, P, B * LQ], BF16).ap()
        mask_scr = nc.dram_tensor("mask_scr", [B, LK], BF16).ap()
        some_scr = nc.dram_tensor("some_scr", [1, B], F32).ap()

        S = stack.enter_context(nc.psum_tensor("S", [P, 4, 512], F32))
        O = stack.enter_context(nc.psum_tensor("O", [P, 2, 512], F32))
        MB = stack.enter_context(nc.psum_tensor("MB", [P, 512], F32))
        XB = stack.enter_context(nc.psum_tensor("XB", [P, 512], F32))

        idn = sb("idn", [P, P], F32)
        xs = sb("xs", [P, TOK, D], F32)
        good = sb("good", [P, QT, HG], F32)
        good_p = sb("good_p", [P, 1], F32)
        good_all = sb("good_all", [1, 1], F32)
        flag = sb("flag", [1, 1], I32)
        hid = sb("hid", [P, TOK, D], F32)
        st = sb("st", [P, TOK, 6], F32)
        mv1 = sb("mv1", [P, TOK, 2], F32)
        mv2 = sb("mv2", [P, TOK, 2], F32)
        rs = sb("rs", [P, 4, TOK], F32)
        cols_s = sb("cols_s", [P, 20], F32)
        rows_s = sb("rows_s", [P, 3, D], F32)
        w_qc_s = sb("w_qc_s", [P, 2, KC, D], F32)
        some = sb("some", [P, B], F32)
        ln1_w, ln1_b, ln2_w, ln2_b = (cols_s[:, 2 * i:2 * i + 2] for i in range(4))
        bq_s, bk_s, fcb_s = cols_s[:, 8:10], cols_s[:, 10:12], cols_s[:, 12:20]
        bv_s, bc_s, pjb_s = (rows_s[:, i, :] for i in range(3))

        mid = ExitStack()
        kst = sb("kst", [P, SLOTS, HG, KP], BF16, mid)
        qst = sb("qst", [P, SLOTS, HG, LQ], BF16, mid)
        vsl = sb("vsl", [P, SLOTS, KT, HG * VW], F32, mid)

        early = ExitStack()
        w_raw = sb("w_raw", [P, 2, KC, D], F32, early)
        w_hi = sb("w_hi", [P, 2, KC, D], F32R, early)
        w_lo = sb("w_lo", [P, 2, KC, D], F32R, early)
        cT = sb("cT", [P, CH, KC, NKM], F32, early)
        c_hi = sb("c_hi", [P, 2, KC, NKM], F32R, early)
        c_lo = sb("c_lo", [P, 2, KC, NKM], F32R, early)
        kpart = sb("kpart", [P, 2, 2, 3, NKM], BF16, early)
        kres = sb("kres", [P, 2, NKM], F32, early)
        vst = sb("vst", [P, 2, SLOTS, max(NT), HG * VW], F32, early)
        ones = sb("ones", [3, KP], BF16, early)
        mk_u = sb("mk_u", [B, LK], U8, early)
        mk_f = sb("mk_f", [B, LK], F32, early)
        mk_b = sb("mk_b", [B, LK], BF16, early)
        some_b = sb("some_b", [B, 2], F32, early)
        qf = sb("qf", [P, 2, TG], F32, early)
        qres = sb("qres", [P, 2, TG], F32, early)
        qpart = sb("qpart", [P, 2, 3, TG], BF16, early)
        early.close()
        xn = hid[:, 0:8, :].rearrange("p (a t) d -> p a t d", a=2)
        xT = hid[:, 8:16, :].rearrange("p (a k u) d -> p a k (u d)", a=2, k=KC)

        late = ExitStack()
        fc_raw = sb("fc_raw", [P, KC, INNER], F32, late)
        pj_raw = sb("pj_raw", [P, NI, D], F32, late)
        fc_hi = sb("fc_hi", [P, KC, INNER], F32R, late)
        fc_lo = sb("fc_lo", [P, KC, INNER], F32R, late)
        pj_hi = sb("pj_hi", [P, NI, D], F32R, late)
        pj_lo = sb("pj_lo", [P, NI, D], F32R, late)
        pr = sb("pr", [P, PBUF, QG], F32, late)
        mxp = sb("mxp", [P, QT, HG, 4], F32, late)
        mx = sb("mx", [P, 2, QT, HG], F32, late)
        mres = sb("mres", [HG, LQ], F32, late)
        mrow = sb("mrow", [HG, 2, 3, LQ], BF16, late)
        osb = sb("osb", [P, 2, LQ], F32, late)
        rec = sb("rec", [P, QT, HG], F32, late)
        att = sb("att", [P, QT, D], F32, late)
        attT = sb("attT", [P, KC, LQ], F32, late)
        late.close()

        mid.close()
        last = ExitStack()
        yn = sb("yn", [P, 2, TT, D], F32, last)
        yT = sb("yT", [P, 2, KC, TG], F32, last)
        y_hi = sb("y_hi", [P, 2, KC, TG], F32R, last)
        y_lo = sb("y_lo", [P, 2, KC, TG], F32R, last)
        g = sb("g", [P, 2, TG], F32, last)
        g_hi = sb("g_hi", [P, NI, TG], F32R, last)
        g_lo = sb("g_lo", [P, NI, TG], F32R, last)
        ob = sb("ob", [P, 2, D], F32, last)
        last.close()

        cols_in, rows_in, wkv_in, wqc_in, idn_in, x_in, mask_in = map(
            sem, ("cols_in", "rows_in", "wkv_in", "wqc_in", "idn_in", "x_in", "mask_in"))
        ctx_in = [sem(f"ctx_in{c}") for c in range(CH)]
        k_out = [sem(f"k_out{i}") for i in range(2)]
        v_out = [sem(f"v_out{i}") for i in range(2)]
        q_out = [sem(f"q_out{i}") for i in range(2)]
        out_done = [sem(f"out_done{i}") for i in range(2)]
        mask_out, some_out, some_in, ones_in, mlpw_in = map(
            sem, ("mask_out", "some_out", "some_in", "ones_in", "mlpw_in"))
        pads_set, w_split, mask_steps = map(sem, ("pads_set", "w_split", "mask_steps"))
        hi_done, lo_done = sem("hi_done"), sem("lo_done")
        k_ready, kh_done, kres_done, km_done, kl_done = map(
            sem, ("k_ready", "kh_done", "kres_done", "km_done", "kl_done"))
        v_ready, v_done = sem("v_ready"), sem("v_done")
        st_steps, var_done, root_done, rstd_steps = map(sem, ("st_steps", "var_done", "root_done", "rstd_steps"))
        good_steps, good_ready, flag_done = map(sem, ("good_steps", "good_ready", "flag_done"))
        xn_done, xt_ready, xt_done, xb_done = map(sem, ("xn_done", "xt_ready", "xt_done", "xb_done"))
        q_ready, qf_done, qh_done, qres_done, qm_done, ql_done = map(
            sem, ("q_ready", "qf_done", "qh_done", "qres_done", "qm_done", "ql_done"))
        o_zeroed = sem("o_zeroed")
        mlpw_hi, mlpw_lo = sem("mlpw_hi"), sem("mlpw_lo")
        yn_done, yt_ready, yt_done, yhi_done, ylo_done = map(
            sem, ("yn_done", "yt_ready", "yt_done", "yhi_done", "ylo_done"))
        fc_ready, g_done, ghi_done, glo_done, pj_ready, ob_half, ob_done = map(
            sem, ("fc_ready", "g_done", "ghi_done", "glo_done", "pj_ready", "ob_half", "ob_done"))
        KRES0 = 4
        V0 = 4
        VR0 = NT[-1] + 1
        KL0 = OUT0 = 1
        EXP0 = 2
        O0 = 2
        ONE = 1

        def section(name, maxima):
            s = Section()
            s.maxima = maxima
            s.uses = HG * len(maxima) + 1
            s.slot_in = [sem(f"{name}_slot_in{i}") for i in range(SLOTS)]
            s.mrow_in = [sem(f"{name}_mrow_in{i}") for i in range(SLOTS)]
            s.scores_done = sem(f"{name}_scores_done")
            s.exp_done = sem(f"{name}_exp_done")
            s.o_ready = sem(f"{name}_o_ready")
            s.o_taken = sem(f"{name}_o_taken")
            s.max_ready = sem(f"{name}_max_ready")
            s.max_taken = sem(f"{name}_max_taken")
            s.mx_done = sem(f"{name}_mx_done")
            s.m_steps = sem(f"{name}_m_steps")
            s.mrow_done = sem(f"{name}_mrow_done")
            s.x_ready = sem(f"{name}_x_ready")
            s.x_taken = sem(f"{name}_x_taken")
            s.rec_done = sem(f"{name}_rec_done")
            s.h_steps = sem(f"{name}_h_steps")
            s.var_done = sem(f"{name}_var_done")
            s.root_done = sem(f"{name}_root_done")
            s.rstd_steps = sem(f"{name}_rstd_steps")
            return s

        XU = SLOTS + 2
        first = section("first", BLOCKKEYS)
        whole = section("whole", ALLKEYS)

        def failed(eng):
            eng.wait_ge(flag_done, 1)
            return eng.If(eng.value_load(flag[0:1, 0:1], min_val=0, max_val=1) < 1)

        block = stack.enter_context(nc.Block())

        def v_bank(kt):
            return (O[:, 0, :], O[:, 1, :], MB[:, :], XB[:, :])[kt % 4]

        @block.sync
        def _(sp):
            def load_ctx(b, c):
                sp.dma_start(cT[:, c, :, 0:NK[c]], ctx_t[bass.ds(b, 1), :, :, T0[c] * P:T0[c] * P + NK[c]]
                             .rearrange("o k p t -> p (o k) t")).then_inc(ctx_in[c], 16)

            def store_kv(b, c):
                i, t, n = c % 2, T0[c] * P, NK[c]
                sp.wait_ge(kl_done, KL0 + 2 * (CH * b + c + 1))
                for mt in range(2):
                    sp.dma_start(k_scr[bass.ds(b, 1), mt, :, :, t:t + n].rearrange("o r p t -> p (o r) t"),
                                 kpart[:, i, mt, :, 0:n]).then_inc(k_out[i], 16)
                sp.wait_ge(v_done, V0 + KT * b + T0[c] + NT[c])
                sp.dma_start(v_scr[bass.ds(b, 1), :, :, T0[c] * HG * VW:(T0[c] + NT[c]) * HG * VW]
                             .rearrange("o s p w -> p (o s) w"),
                             vst[:, i, :, 0:NT[c], :].rearrange("p s t w -> p s (t w)")).then_inc(v_out[i], 16)

            for i in range(2):
                sp.sem_inc(k_out[i], OUT0)
                sp.sem_inc(v_out[i], OUT0)
            for s_ in (first, whole):
                for s in range(SLOTS):
                    sp.sem_inc(s_.mrow_in[s], ONE)
            sp.dma_start(w_raw[:], w_kv).then_inc(wkv_in, 16)
            for c in range(CH):
                load_ctx(0, c)
            sp.dma_start(w_qc_s[:], w_qc).then_inc(wqc_in, 16)
            sp.wait_ge(mask_steps, 4)
            sp.dma_start(mask_scr, mk_b[:]).then_inc(mask_out, 16)
            sp.dma_start(some_scr.rearrange("o b -> b o"), some_b[:, 1:2]).then_inc(some_out, 16)
            sp.wait_ge(some_out, 16)
            sp.dma_start(some[:], some_scr[0].partition_broadcast(P)).then_inc(some_in, 16)
            sp.wait_ge(pads_set, 5)
            sp.dma_start(kst[MAXROW:MAXROW + 3, :, :, :].rearrange("p s h t -> p (s h) t"),
                         ones[:].unsqueeze(1).broadcast_to([3, H, KP])).then_inc(ones_in, 16)
            sp.dma_start(qst[MASKROW:MASKROW + 1, :, :, :].rearrange("p s h t -> p (s h) t"),
                         ones[0:1, 0:LQ].unsqueeze(1).broadcast_to([1, H, LQ])).then_inc(ones_in, 16)
            with sp.Fori(0, B - 1) as b:
                for c in range(CH):
                    sp.wait_ge(lo_done, CH * b + c + 1)
                    load_ctx(b + 1, c)
                    store_kv(b, c)
            for c in range(CH):
                store_kv(B - 1, c)

            def fill_kv(s_, b, s):
                rows_of = k_scr[bass.ds(b, 1), s // 2].rearrange("o r (d h) t -> (o r d) h t", h=HM)[
                    :, HG * (s % 2):HG * (s % 2) + HG, 0:LK]
                for r0, parts in ((0, 3), (3 * HD, 2), (5 * HD, 1)):
                    sp.dma_start(kst[r0:r0 + parts * HD, s, :, 0:LK], rows_of[0:parts * HD]
                                 ).then_inc(s_.slot_in[s], 16)
                sp.dma_start(kst[MASKROW:MASKROW + 1, s, :, 0:LK],
                             mask_scr[bass.ds(b, 1), :].unsqueeze(1).broadcast_to([1, HG, LK])
                             ).then_inc(s_.slot_in[s], 16)
                sp.dma_start(vsl[:, s, :, :].rearrange("p t w -> p (t w)"),
                             v_scr[bass.ds(b, 1), s].rearrange("o p w -> (o p) w")).then_inc(s_.slot_in[s], 16)

            def fill_q(s_, b, s):
                sp.dma_start(qst[0:ROWS, s, :, :], q_scr[s // 2].rearrange("g (d h) q -> (g d) h q", h=HM)[
                    :, HG * (s % 2):HG * (s % 2) + HG, bass.ds(b * LQ, LQ)]).then_inc(s_.slot_in[s], 16)

            for i in range(2):
                sp.wait_ge(k_out[i], OUT0 + 16 * 2 * B * CH // 2)
                sp.wait_ge(v_out[i], OUT0 + 16 * B * CH // 2)
            sp.wait_ge(mask_out, 16)
            sp.wait_ge(ones_in, 32)
            for s in range(SLOTS - 1):
                fill_kv(first, 0, s)
            for j in range(2 * NTG):
                sp.wait_ge(ql_done, j + 1)
                dst = q_scr[j % 2, :, :, j // 2 * TG:(j // 2 + 1) * TG].rearrange("g p q -> p g q")
                for part, g0, ng in ((0, 0, 3), (1, 3, 2), (2, 5, 1)):
                    sp.dma_start(dst[:, g0:g0 + ng, :], qpart[:, j % 2, part:part + 1, :].broadcast_to([P, ng, TG])
                                 ).then_inc(q_out[j % 2], 16)
            for i in range(2):
                sp.wait_ge(q_out[i], 16 * 3 * NTG)
            for s in range(SLOTS - 1):
                fill_q(first, 0, s)

            def send_rows(s_, b, s):
                sp.wait_ge(s_.mrow_done, SLOTS * b + s + 1)
                for part in range(3):
                    r = MAXROW + part
                    sp.dma_start(qst[r:r + 1, s, :, :], mrow[:, s % 2, part, :]).then_inc(s_.mrow_in[s], 16)

            def attention(s_, b, final):
                for s in range(SLOTS):
                    if s == 0 or not final:
                        sp.wait_ge(s_.o_ready, ONE + SLOTS * b + s)
                        fill_kv(s_, b if s == 0 else b + 1, (s + 3) % SLOTS)
                        fill_q(s_, b if s == 0 else b + 1, (s + 3) % SLOTS)
                    if s < 2 or not final:
                        send_rows(s_, b if s < 2 else b + 1, (s + 2) % SLOTS)

            send_rows(first, 0, 0)
            send_rows(first, 0, 1)
            attention(first, 0, False)
            sp.dma_start(fc_raw[:], fc).then_inc(mlpw_in, 16)
            sp.dma_start(pj_raw[:], pj).then_inc(mlpw_in, 16)
            with sp.Fori(1, B - 1) as b:
                attention(first, b, False)
            attention(first, B - 1, True)
            with failed(sp):
                with sp.Fori(0, B) as b:
                    sp.wait_ge(whole.o_ready, ONE + SLOTS * b)
                    for s in range(SLOTS - 1):
                        fill_kv(whole, b, s)
                        fill_q(whole, b, s)
                    send_rows(whole, b, 0)
                    send_rows(whole, b, 1)
                    attention(whole, b, True)

            for t in range(TOK):
                sp.wait_ge(ob_done, t + 1)
                sp.dma_start(out[t * P:(t + 1) * P, :], ob[:, t % 2, :]).then_inc(out_done[t % 2], 16)
            for i in range(2):
                sp.wait_ge(out_done[i], 16 * TOK // 2)

        @block.gpsimd
        def _(pool):
            nc.gpsimd.memset(ones[:], 1.0).then_inc(pads_set, 1)
            nc.gpsimd.memset(cT[:, CH - 1, :, NK[-1]:NKM], 0.0).then_inc(pads_set, 1)
            nc.gpsimd.memset(vst[:], 1.0).then_inc(pads_set, 1)
            pool.wait_ge(pads_set, 3)
            nc.gpsimd.memset(vst[64:P, 1, :, NT[-1] - 1, :], 0.0).then_inc(pads_set, 1)
            pool.wait_ge(pads_set, 4)
            nc.gpsimd.memset(kst[:, :, :, LK:KP], 0.0).then_inc(pads_set, 1)
            pool.wait_ge(pads_set, 5)
            nc.gpsimd.memset(vst[64:TAIL, 1, :, NT[-1] - 1, :], 1.0).then_inc(pads_set, 1)

            with pool.Fori(0, B) as b:
                for c in range(CH):
                    pool.wait_ge(hi_done, CH * b + c + 1)
                    i, n = c % 2, NKE[c]
                    nc.gpsimd.tensor_tensor(c_lo[:, i, :, 0:n], cT[:, c, :, 0:n], c_hi[:, i, :, 0:n].bitcast(F32),
                                            ALU.subtract).then_inc(lo_done, 1)
            pool.wait_ge(rows_in, 16)
            pool.wait_ge(xn_done, TOK)
            nc.gpsimd.tensor_tensor(xs[:], xs[:], bc_s.unsqueeze(1).broadcast_to([P, TOK, D]),
                                    ALU.add).then_inc(xb_done, 1)

            pool.wait_ge(mlpw_in, 32)
            nc.gpsimd.tensor_copy(fc_hi[:], fc_raw[:]).then_inc(mlpw_hi, 1)
            nc.gpsimd.tensor_copy(pj_hi[:], pj_raw[:]).then_inc(mlpw_hi, 1)
            with failed(pool):
                pool.nop()
            pool.wait_ge(mlpw_hi, 2)
            nc.gpsimd.tensor_tensor(fc_lo[:], fc_raw[:], fc_hi[:].bitcast(F32), ALU.subtract).then_inc(mlpw_lo, 1)
            nc.gpsimd.tensor_tensor(pj_lo[:], pj_raw[:], pj_hi[:].bitcast(F32), ALU.subtract).then_inc(mlpw_lo, 1)
            for c in range(NTG):
                pool.wait_ge(yhi_done, c + 1)
                if c >= 2:
                    pool.wait_ge(fc_ready, NI * (c - 1))
                nc.gpsimd.tensor_tensor(y_lo[:, c % 2], yT[:, c % 2], y_hi[:, c % 2].bitcast(F32),
                                        ALU.subtract).then_inc(ylo_done, 1)

        @block.scalar
        def _(act):
            act.dma_start(mk_u[:], mask).then_inc(mask_in, 16)
            act.dma_start(cols_s[:], cols).then_inc(cols_in, 16)
            act.dma_start(rows_s[:], rows.partition_broadcast(P)).then_inc(rows_in, 16)
            for i in range(2):
                act.dma_start(xs[:, 8 * i:8 * i + 8, :], x[8 * i:8 * i + 8].rearrange("n p d -> p n d")
                              ).then_inc(x_in, 16)
            act.dma_start(idn[:], ident).then_inc(idn_in, 16)

            two_back = [T0[CH - 1] - KT, 0] + T0[1:CH - 1]

            def high(b, c):
                act.wait_ge(ctx_in[c], 16 * (b + 1))
                act.wait_ge(v_ready, VR0 + KT * b + two_back[c])
                nc.scalar.activation(c_hi[:, c % 2, :, 0:NKE[c]], cT[:, c, :, 0:NKE[c]], ACT.Copy
                                     ).then_inc(hi_done, 1)

            def k_parts(b, c):
                i, n = c % 2, NK[c]
                act.wait_ge(k_out[i], OUT0 + 16 * 2 * (2 * b + c // 2))
                for mt in range(2):
                    j = 2 * c + mt
                    act.wait_ge(k_ready, 2 * CH * b + j + 1)
                    nc.scalar.activation(kpart[:, i, mt, 0, 0:n], S[:, j % 4, 0:n], ACT.Identity,
                                         bias=bk_s[:, mt:mt + 1]).then_inc(kh_done, 1)
                for mt in range(2):
                    act.wait_ge(kres_done, KRES0 + 2 * (CH * b + c) + mt + 1)
                    nc.scalar.activation(kpart[:, i, mt, 1, 0:n], kres[:, mt, 0:n], ACT.Copy).then_inc(km_done, 1)

            act.wait_ge(cols_in, 16)
            act.wait_ge(pads_set, 6)
            high(0, 0)
            with act.Fori(0, B - 1) as b:
                for c in range(CH):
                    high(b if c + 1 < CH else b + 1, (c + 1) % CH)
                    k_parts(b, c)
            for c in range(CH):
                if c + 1 < CH:
                    high(B - 1, c + 1)
                k_parts(B - 1, c)

            act.wait_ge(var_done, 1)
            nc.scalar.activation(rs[:, 1, :], rs[:, 0, :], ACT.Sqrt).then_inc(root_done, 1)

            def x_t(t):
                for k in range(KC):
                    act.wait_ge(xt_ready, KC * t + k + 1)
                    if t >= 2:
                        act.wait_ge(q_ready, 2 * (t - 1))
                    nc.scalar.activation(xT[:, t % 2, k, :], S[:, k, :], ACT.Identity,
                                         bias=ln1_b[:, k:k + 1], scale=ln1_w[:, k:k + 1]).then_inc(xt_done, 1)

            def q_parts(j):
                if j >= 2:
                    act.wait_ge(q_out[j % 2], 16 * 3 * (j // 2))
                act.wait_ge(qf_done, j + 1)
                nc.scalar.activation(qpart[:, j % 2, 0, :], qf[:, j % 2, :], ACT.Copy).then_inc(qh_done, 1)
                act.wait_ge(qres_done, j + 1)
                nc.scalar.activation(qpart[:, j % 2, 1, :], qres[:, j % 2, :], ACT.Copy).then_inc(qm_done, 1)

            for t in range(NTG + 1):
                if t < NTG:
                    x_t(t)
                if t >= 1:
                    q_parts(2 * (t - 1))
                    q_parts(2 * (t - 1) + 1)

            assert PBUF >= LAG + 2 and (SLOTS * KT) % PBUF == 0 and (SLOTS * KT) % 2 == 0

            def attention(s_, b):
                for n in range(SLOTS * KT):
                    act.wait_ge(s_.scores_done, SLOTS * KT * b + n + 1)
                    nc.scalar.activation(pr[:, n % PBUF, :], S[:, 2 * (n % 2):2 * (n % 2) + 2, :]
                                         .rearrange("p a n -> p (a n)"), ACT.Exp).then_inc(s_.exp_done, 1)

            def root(s_):
                act.wait_ge(s_.var_done, 1)
                nc.scalar.activation(rs[:, 1, :], rs[:, 0, :], ACT.Sqrt).then_inc(s_.root_done, 1)

            act.sem_inc(first.exp_done, EXP0)
            act.sem_inc(whole.exp_done, EXP0)
            with act.Fori(0, B) as b:
                attention(first, b)
            root(first)
            with failed(act):
                with act.Fori(0, B) as b:
                    attention(whole, b)
                root(whole)


            def y_t(c):
                for k in range(KC):
                    act.wait_ge(yt_ready, KC * c + k + 1)
                    if c >= 2:
                        act.wait_ge(ylo_done, c - 1)
                    nc.scalar.activation(yT[:, c % 2, k, :], (MB, XB)[k][:, :], ACT.Identity,
                                         bias=ln2_b[:, k:k + 1], scale=ln2_w[:, k:k + 1]).then_inc(yt_done, 1)

            y_t(0)
            for c in range(NTG):
                for i in range(NI):
                    j = NI * c + i
                    act.wait_ge(fc_ready, j + 1)
                    if j >= 2:
                        act.wait_ge(glo_done, j - 1)
                    nc.scalar.activation(g[:, j % 2, :], S[:, j % 4, :], ACT.Gelu_apprx_tanh,
                                         bias=fcb_s[:, i:i + 1]).then_inc(g_done, 1)
                    if i == 4 and c + 1 < NTG:
                        y_t(c + 1)

        @block.vector
        def _(dve):
            dve.sem_inc(kres_done, KRES0)
            dve.sem_inc(kl_done, KL0)
            dve.sem_inc(v_done, V0)
            for s_ in (first, whole):
                dve.sem_inc(s_.o_taken, O0)
                dve.sem_inc(s_.max_taken, ONE)
                dve.sem_inc(s_.x_taken, ONE)
            nc.vector.memset(good[:], 1.0).then_inc(good_steps, 1)
            dve.wait_ge(wkv_in, 16)
            nc.vector.tensor_copy(w_hi[:], w_raw[:]).then_inc(w_split, 1)
            dve.wait_ge(w_split, 1)
            nc.vector.tensor_tensor(w_lo[:], w_raw[:], w_hi[:].bitcast(F32), ALU.subtract).then_inc(w_split, 1)
            dve.wait_ge(mask_in, 16)
            nc.vector.tensor_copy(mk_f[:], mk_u[:]).then_inc(mask_steps, 1)
            dve.wait_ge(mask_steps, 1)
            nc.vector.tensor_reduce(some_b[:, 0:1], mk_f[:], AX.X, ALU.max).then_inc(mask_steps, 1)
            dve.wait_ge(mask_steps, 2)
            nc.vector.tensor_scalar(mk_b[:], mk_f[:], some_b[:, 0:1], MASKED, ALU.subtract, ALU.mult
                                    ).then_inc(mask_steps, 1)
            nc.vector.tensor_scalar(some_b[:, 1:2], some_b[:, 0:1], SCALE, None, ALU.mult).then_inc(mask_steps, 1)

            def k_rest(b, c):
                i, n = c % 2, NK[c]
                dve.wait_ge(kl_done, KL0 + 2 * (CH * b + c))
                for mt in range(2):
                    j = 2 * c + mt
                    dve.wait_ge(kh_done, 2 * CH * b + j + 1)
                    nc.vector.scalar_tensor_tensor(out=kres[:, mt, 0:n], in0=S[:, j % 4, 0:n],
                                                   scalar=bk_s[:, mt:mt + 1], in1=kpart[:, i, mt, 0, 0:n],
                                                   op0=ALU.add, op1=ALU.subtract).then_inc(kres_done, 1)

            def k_low(b, c):
                i, n = c % 2, NK[c]
                for mt in range(2):
                    dve.wait_ge(km_done, 2 * (CH * b + c) + mt + 1)
                    nc.vector.tensor_tensor(kpart[:, i, mt, 2, 0:n], kres[:, mt, 0:n], kpart[:, i, mt, 1, 0:n],
                                            ALU.subtract).then_inc(kl_done, 1)

            def v_tiles(b, c):
                dve.wait_ge(v_out[c % 2], OUT0 + 16 * (2 * b + c // 2))
                for t in range(NT[c]):
                    kt = T0[c] + t
                    m = TAIL if kt == KT - 1 else P
                    dve.wait_ge(v_ready, VR0 + KT * b + kt + 1)
                    nc.vector.tensor_tensor(
                        vst[0:m, c % 2, :, t, :].rearrange("p s (h w) -> p s h w", w=VW)[:, :, :, 0:HD],
                        v_bank(kt)[0:m, 0:D].rearrange("p (s h d) -> p s h d", s=SLOTS, d=HD),
                        bv_s[0:m, :].rearrange("p (s h d) -> p s h d", s=SLOTS, d=HD), ALU.add).then_inc(v_done, 1)

            dve.wait_ge(cols_in, 16)
            dve.wait_ge(rows_in, 16)
            dve.wait_ge(x_in, 32)
            dve.wait_ge(pads_set, 6)
            with dve.Fori(0, B) as b:
                for c in range(CH):
                    k_rest(b, c)
                    k_low(b, c)
                    v_tiles(b, c)
                for q in range(QT):
                    nc.vector.bn_stats(st[:, bass.ds(QT * b + q, 1), :], xs[:, bass.ds(QT * b + q, 1), :]
                                       ).then_inc(st_steps, 1)

            def moments(mv, tiles, steps):
                for n in tiles:
                    nc.vector.bn_aggr(mv[:, n, :], st[:, n, :]).then_inc(steps, 1)

            def rstd(mv, rstd_steps, var_done, root_done):
                before = TOK
                dve.wait_ge(rstd_steps, before)
                nc.vector.tensor_scalar(rs[:, 0, :], mv[:, :, 1], EPS, None, ALU.add).then_inc(var_done, 1)
                dve.wait_ge(root_done, 1)
                nc.vector.reciprocal(rs[:, 2, :], rs[:, 1, :]).then_inc(rstd_steps, 1)
                dve.wait_ge(rstd_steps, before + 1)
                nc.vector.tensor_tensor(rs[:, 3, :], rs[:, 0, :], rs[:, 2, :], ALU.mult).then_inc(rstd_steps, 1)
                dve.wait_ge(rstd_steps, before + 2)
                nc.vector.tensor_tensor(rs[:, 3, :], rs[:, 3, :], rs[:, 2, :], ALU.mult).then_inc(rstd_steps, 1)
                dve.wait_ge(rstd_steps, before + 3)
                nc.vector.tensor_scalar(rs[:, 3, :], rs[:, 3, :], -0.5, 1.5, ALU.mult, ALU.add
                                        ).then_inc(rstd_steps, 1)
                dve.wait_ge(rstd_steps, before + 4)
                nc.vector.tensor_tensor(rs[:, 2, :], rs[:, 2, :], rs[:, 3, :], ALU.mult).then_inc(rstd_steps, 1)
                dve.wait_ge(rstd_steps, before + 5)

            def normalise(dst, src, mv, t, done, read):
                if t >= 2:
                    dve.wait_ge(read, KC * (t - 1))
                for i in range(TT):
                    n = TT * t + i
                    nc.vector.tensor_scalar(dst[:, t % 2, i, :], src[:, n, :], mv[:, n, 0:1], rs[:, 2, n:n + 1],
                                            ALU.subtract, ALU.mult).then_inc(done, 1)

            def q_rest(j):
                i, t = j % 2, j // 2
                dve.wait_ge(q_ready, j + 1)
                for half in range(TG // LQ):
                    b = TG // LQ * t + half
                    last = nc.vector.tensor_scalar(
                        qf[:, i, half * LQ:(half + 1) * LQ], S[:, 2 + i, half * LQ:(half + 1) * LQ],
                        bq_s[:, i:i + 1], some[:, b:b + 1], ALU.add, ALU.mult)
                last.then_inc(qf_done, 1)
                dve.wait_ge(qh_done, j + 1)
                nc.vector.tensor_tensor(qres[:, i, :], qf[:, i, :], qpart[:, i, 0, :], ALU.subtract
                                        ).then_inc(qres_done, 1)
                dve.wait_ge(qm_done, j + 1)
                nc.vector.tensor_tensor(qpart[:, i, 2, :], qres[:, i, :], qpart[:, i, 1, :], ALU.subtract
                                        ).then_inc(ql_done, 1)

            dve.wait_ge(st_steps, TOK)
            moments(mv1, range(TOK), rstd_steps)
            rstd(mv1, rstd_steps, var_done, root_done)
            dve.wait_ge(some_in, 16)
            normalise(xn, xs, mv1, 0, xn_done, xt_ready)
            for t in range(NTG):
                if t + 1 < NTG:
                    normalise(xn, xs, mv1, t + 1, xn_done, xt_ready)
                q_rest(2 * t)
                q_rest(2 * t + 1)

            nc.vector.memset(O[:, :, 0:LQ], 0.0).then_inc(o_zeroed, 1)

            def maxima_of(s_, n, s, h):
                for i, products in enumerate(s_.maxima):
                    use = s_.uses * n + h * len(s_.maxima) + i
                    dve.wait_ge(s_.max_ready, use + 1)
                    if s_ is first:
                        nc.vector.tensor_reduce(mx[:, s % 2, :, h], MB[:, :].rearrange("p (q k) -> p q k", q=QT),
                                                AX.X, ALU.max, negate=True).then_inc(s_.max_taken, 1)
                    else:
                        _, q, k, w = products[0]
                        nc.vector.tensor_reduce(mxp[:, q, h, i % 4:i % 4 + 1], MB[:, 0:w], AX.X, ALU.max
                                                ).then_inc(s_.max_taken, 1)
                if s_ is whole and h == HG - 1:
                    dve.wait_ge(s_.max_taken, ONE + s_.uses * n + HG * len(s_.maxima))
                    nc.vector.tensor_reduce(mx[:, s % 2], mxp[:], AX.X, ALU.max, negate=True
                                            ).then_inc(s_.mx_done, 1)

            def max_rows(s_, n, b, s):
                dve.wait_ge(s_.max_ready, s_.uses * (n + 1))
                dve.wait_ge(s_.mrow_in[(s + 2) % SLOTS], ONE + 16 * 3 * (b if s < 2 else b + 1))
                hi, mi, lo = (mrow[:, s % 2, part, :] for part in range(3))
                nc.vector.tensor_copy(hi, MB[0:HG, 0:LQ]).then_inc(s_.m_steps, 1)
                dve.wait_ge(s_.m_steps, 2 * n + 1)
                nc.vector.tensor_tensor(mres[:], MB[0:HG, 0:LQ], hi, ALU.subtract).then_inc(s_.max_taken, 1)
                dve.wait_ge(s_.max_taken, ONE + s_.uses * (n + 1))
                nc.vector.tensor_copy(mi, mres[:]).then_inc(s_.m_steps, 1)
                dve.wait_ge(s_.m_steps, 2 * n + 2)
                nc.vector.tensor_tensor(lo, mres[:], mi, ALU.subtract).then_inc(s_.mrow_done, 1)

            def take_o(s_, n, s):
                dve.wait_ge(s_.o_ready, ONE + n + 1)
                nc.vector.tensor_copy(osb[:, s % 2, :], O[:, s % 2, 0:LQ]).then_inc(s_.o_taken, 1)

            def divide(s_, b, n, s):
                dve.wait_ge(s_.x_ready, XU * b + s + 1)
                ot = XB[:, 0:QT * P].rearrange("p (q h w) -> p q h w", q=QT, w=32)
                nc.vector.reciprocal(rec[:], ot[:, :, :, HD]).then_inc(s_.rec_done, 1)
                if s_ is first:
                    dve.wait_ge(good_steps, n + 1)
                    nc.vector.scalar_tensor_tensor(out=good[:], in0=ot[:, :, :, HD], scalar=LARGE, in1=good[:],
                                                   op0=ALU.is_lt, op1=ALU.mult).then_inc(good_steps, 1)
                dve.wait_ge(s_.rec_done, n + 1)
                nc.vector.tensor_tensor(
                    att[:, :, s * HG * HD:(s + 1) * HG * HD].rearrange("p q (h d) -> p q h d", d=HD),
                    ot[:, :, :, 0:HD], rec[:].unsqueeze(3).broadcast_to([P, QT, HG, HD]), ALU.mult
                ).then_inc(s_.x_taken, 1)

            def take_att_t(s_, b):
                dve.wait_ge(s_.x_ready, XU * b + SLOTS + 1)
                nc.vector.tensor_copy(attT[:].rearrange("p k q -> p (k q)"), XB[:, :]).then_inc(s_.x_taken, 1)

            def hidden(s_, b):
                dve.wait_ge(s_.x_ready, XU * b + SLOTS + 2)
                rows_ = bass.ds(QT * b, QT)
                nc.vector.tensor_tensor(hid[:, rows_, :], XB[:, :].rearrange("p (q d) -> p q d", q=QT),
                                        xs[:, rows_, :], ALU.add).then_inc(s_.x_taken, 1)
                dve.wait_ge(s_.x_taken, ONE + XU * (b + 1))
                for q in range(QT):
                    last = nc.vector.bn_stats(st[:, bass.ds(QT * b + q, 1), :], hid[:, bass.ds(QT * b + q, 1), :])
                last.then_inc(s_.h_steps, 1)

            def attention(s_, b, start, final):
                for s in range(SLOTS):
                    n = SLOTS * b + s
                    b2 = b if s < 2 else b + 1
                    s2 = (s + 2) % SLOTS
                    before = not (start and s == 0)
                    ahead = s < 2 or not final
                    if ahead:
                        maxima_of(s_, n + 2, s2, 0)
                    if before:
                        take_o(s_, n - 1, (s - 1) % SLOTS)
                    if ahead:
                        maxima_of(s_, n + 2, s2, 1)
                    if before:
                        divide(s_, b if s else b - 1, n - 1, (s - 1) % SLOTS)
                    if ahead:
                        maxima_of(s_, n + 2, s2, 2)
                        maxima_of(s_, n + 2, s2, 3)
                    if before and s == 0:
                        take_att_t(s_, b - 1)
                    if ahead:
                        max_rows(s_, n + 2, b2, s2)
                    if before and s == 0:
                        hidden(s_, b - 1)

            def finish(s_, b):
                take_o(s_, SLOTS * (b + 1) - 1, SLOTS - 1)
                divide(s_, b, SLOTS * (b + 1) - 1, SLOTS - 1)
                take_att_t(s_, b)
                hidden(s_, b)

            def prepare(s_, b):
                for s in range(2):
                    for h in range(HG):
                        maxima_of(s_, SLOTS * b + s, s, h)
                    max_rows(s_, SLOTS * b + s, b, s)

            def hidden_rstd(s_):
                dve.wait_ge(s_.h_steps, B)
                moments(mv2, range(TOK), s_.rstd_steps)
                rstd(mv2, s_.rstd_steps, s_.var_done, s_.root_done)

            prepare(first, 0)
            dve.wait_ge(xb_done, 1)
            attention(first, 0, True, False)
            with dve.Fori(1, B - 1) as b:
                attention(first, b, False, False)
            attention(first, B - 1, False, True)
            finish(first, B - 1)
            dve.wait_ge(good_steps, SLOTS * B + 1)
            nc.vector.tensor_reduce(good_p[:], good[:], AX.XY, ALU.min).then_inc(good_steps, 1)
            dve.wait_ge(good_ready, 1)
            nc.vector.tensor_reduce(good_all[:], MB[0:1, 0:P], AX.X, ALU.min).then_inc(good_steps, 1)
            dve.wait_ge(good_steps, SLOTS * B + 3)
            nc.vector.tensor_copy(flag[:], good_all[:]).then_inc(flag_done, 1)
            hidden_rstd(first)
            with failed(dve):
                with dve.Fori(0, B) as b:
                    prepare(whole, b)
                    attention(whole, b, True, True)
                    finish(whole, b)
                hidden_rstd(whole)

            normalise(yn, hid, mv2, 0, yn_done, yt_ready)

            def y_high(c):
                dve.wait_ge(yt_done, KC * (c + 1))
                if c >= 2:
                    dve.wait_ge(fc_ready, NI * (c - 1))
                nc.vector.tensor_copy(y_hi[:, c % 2], yT[:, c % 2]).then_inc(yhi_done, 1)

            y_high(0)
            for c in range(NTG):
                for i in range(NI):
                    j = NI * c + i
                    dve.wait_ge(g_done, j + 1)
                    nc.vector.tensor_copy(g_hi[:, i, :], g[:, j % 2, :]).then_inc(ghi_done, 1)
                    dve.wait_ge(ghi_done, j + 1)
                    nc.vector.tensor_tensor(g_lo[:, i, :], g[:, j % 2, :], g_hi[:, i, :].bitcast(F32), ALU.subtract
                                            ).then_inc(glo_done, 1)
                    if i == 1 and c + 1 < NTG:
                        normalise(yn, hid, mv2, c + 1, yn_done, yt_ready)
                    if i == 6 and c + 1 < NTG:
                        y_high(c + 1)
                for t in range(TT):
                    n = TT * c + t
                    dve.wait_ge(pj_ready, n + 1)
                    if n >= 2:
                        dve.wait_ge(out_done[n % 2], 16 * (n // 2))
                    nc.vector.tensor_tensor(ob[:, n % 2, :], O[:, n % 2, 0:D], pjb_s, ALU.add).then_inc(ob_half, 1)
                    dve.wait_ge(ob_half, n + 1)
                    nc.vector.tensor_tensor(ob[:, n % 2, :], ob[:, n % 2, :], hid[:, n, :], ALU.add
                                            ).then_inc(ob_done, 1)

        @block.tensor
        def _(pe):
            def product3(dst, w, m):
                terms = [(a, c) for (wh, wl), (mh, ml) in zip(w, m) for a, c in ((wh, mh), (wh, ml), (wl, mh))]
                for i, (a, c) in enumerate(terms):
                    last = nc.tensor.matmul(dst, a, c, start=i == 0, stop=i == len(terms) - 1)
                return last

            pe.sem_inc(v_ready, VR0)
            pe.sem_inc(first.o_ready, ONE)
            pe.sem_inc(whole.o_ready, ONE)
            pe.wait_ge(w_split, 2)
            with pe.Fori(0, B) as b:
                for c in range(CH):
                    i, n = c % 2, NKE[c]
                    pe.wait_ge(lo_done, CH * b + c + 1)
                    for mt in range(2):
                        j = 2 * c + mt
                        pe.wait_ge(kres_done, 2 * CH * b + j + 1)
                        cut = slice(mt * P, (mt + 1) * P)
                        product3(S[:, j % 4, 0:n], [(w_hi[:, 0, k, cut], w_lo[:, 0, k, cut]) for k in range(KC)],
                                 [(c_hi[:, i, k, 0:n], c_lo[:, i, k, 0:n]) for k in range(KC)]
                                 ).then_inc(k_ready, 1)
                    for t in range(NT[c]):
                        kt = T0[c] + t
                        m = TAIL if kt == KT - 1 else P
                        pe.wait_ge(v_done, KT * b + (V0 if kt == 0 else kt if kt < 4 else kt + 1))
                        cut = slice(t * P, t * P + m)
                        product3(v_bank(kt)[0:m, 0:D], [(c_hi[:, i, k, cut], c_lo[:, i, k, cut]) for k in range(KC)],
                                 [(w_hi[:, 1, k, :], w_lo[:, 1, k, :]) for k in range(KC)]).then_inc(v_ready, 1)

            pe.wait_ge(idn_in, 16)
            pe.wait_ge(wqc_in, 16)
            pe.wait_ge(kres_done, KRES0 + 2 * CH * B)

            def turn(dst, src, t, normed, taken, ready):
                for i in range(TT):
                    pe.wait_ge(normed, TT * t + i + 1)
                    for k in range(KC):
                        if t >= 1 and i == 0:
                            pe.wait_ge(taken, KC * (t - 1) + k + 1)
                        last = nc.tensor.transpose(dst[k][:, i * P:(i + 1) * P],
                                                   src[:, t % 2, i, k * P:(k + 1) * P], idn[:])
                        if i == TT - 1:
                            last.then_inc(ready, 1)

            def q_product(t):
                for mt in range(2):
                    j = 2 * t + mt
                    pe.wait_ge(xt_done, KC * (t + 1))
                    if j >= 2:
                        pe.wait_ge(qf_done, j - 1)
                    for k in range(KC):
                        last = nc.tensor.matmul(S[:, 2 + mt, :], w_qc_s[:, 0, k, mt * P:(mt + 1) * P],
                                                xT[:, t % 2, k, :], start=k == 0, stop=k == KC - 1)
                    last.then_inc(q_ready, 1)

            turn((S[:, 0, :], S[:, 1, :]), xn, 0, xn_done, xt_done, xt_ready)
            for t in range(NTG):
                if t + 1 < NTG:
                    turn((S[:, 0, :], S[:, 1, :]), xn, t + 1, xn_done, xt_done, xt_ready)
                q_product(t)

            def maxima_of(s_, n, b, s, h):
                if h == 0:
                    pe.wait_ge(s_.slot_in[s], 16 * 6 * (b + 1))
                for i, products in enumerate(s_.maxima):
                    pe.wait_ge(s_.max_taken, ONE + s_.uses * n + h * len(s_.maxima) + i)
                    for col, q, k, w in products:
                        last = nc.tensor.matmul(MB[:, col:col + w], qst[0:MASKROW + 1, s, h, q * P:(q + 1) * P],
                                                kst[0:MASKROW + 1, s, h, k:k + w], start=True, stop=True)
                    last.then_inc(s_.max_ready, 1)

            def max_rows(s_, n, s):
                pe.wait_ge(s_.max_taken, ONE + s_.uses * (n + 1) - 1)
                if s_ is whole:
                    pe.wait_ge(s_.mx_done, n + 1)
                for q in range(QT):
                    last = nc.tensor.matmul(MB[0:HG, q * P:(q + 1) * P], mx[:, s % 2, q, :], idn[:],
                                            start=True, stop=True)
                last.then_inc(s_.max_ready, 1)

            def scores(s_, b, s, kt):
                n = s * KT + kt
                if kt == 0:
                    pe.wait_ge(s_.mrow_in[s], ONE + 16 * 3 * (b + 1))
                pe.wait_ge(s_.exp_done, SLOTS * KT * b + n + 1)
                for h in range(HG):
                    last = nc.tensor.matmul(S[:, 2 * (n % 2) + h // 2, (h % 2) * LQ:(h % 2 + 1) * LQ],
                                            kst[0:KROWS, s, h, kt * P:(kt + 1) * P], qst[0:KROWS, s, h, :],
                                            start=True, stop=True)
                last.then_inc(s_.scores_done, 1)

            def values(s_, b, s, kt):
                if kt == 0:
                    pe.wait_ge(s_.o_taken, SLOTS * b + s + 1)
                for h in range(HG):
                    last = nc.tensor.matmul(O[32 * h:32 * h + VW, s % 2, 0:LQ], vsl[:, s, kt, h * VW:(h + 1) * VW],
                                            pr[:, (s * KT + kt) % PBUF, h * LQ:(h + 1) * LQ],
                                            start=kt == 0, stop=kt == KT - 1, skip_group_check=True)
                if kt == KT - 1:
                    last.then_inc(s_.o_ready, 1)

            def turn_o(s_, b, n, s):
                pe.wait_ge(s_.o_taken, O0 + n + 1)
                pe.wait_ge(s_.x_taken, ONE + XU * b + s)
                for q in range(QT):
                    last = nc.tensor.transpose(XB[:, q * P:(q + 1) * P], osb[:, s % 2, q * P:(q + 1) * P], idn[:])
                last.then_inc(s_.x_ready, 1)

            def turn_att(s_, b):
                pe.wait_ge(s_.x_taken, ONE + XU * b + SLOTS)
                for k in range(KC):
                    for q in range(QT):
                        last = nc.tensor.transpose(XB[:, k * LQ + q * P:k * LQ + (q + 1) * P],
                                                   att[:, q, k * P:(k + 1) * P], idn[:])
                last.then_inc(s_.x_ready, 1)

            def project(s_, b):
                pe.wait_ge(s_.x_taken, ONE + XU * b + SLOTS + 1)
                for q in range(QT):
                    for k in range(KC):
                        last = nc.tensor.matmul(XB[:, q * D:(q + 1) * D], attT[:, k, q * P:(q + 1) * P],
                                                w_qc_s[:, 1, k, :], start=k == 0, stop=k == KC - 1)
                last.then_inc(s_.x_ready, 1)

            def attention(s_, b, start, final):
                for s in range(SLOTS):
                    n = SLOTS * b + s
                    b2 = b if s < 2 else b + 1
                    s2 = (s + 2) % SLOTS
                    before = not (start and s == 0)
                    ahead = s < 2 or not final
                    for kt in range(KT):
                        scores(s_, b, s, kt)
                        if ahead and kt in MAXSTEPS:
                            maxima_of(s_, n + 2, b2, s2, MAXSTEPS.index(kt))
                        if before and kt == 4:
                            turn_o(s_, b if s else b - 1, n - 1, (s - 1) % SLOTS)
                        if before and s == 0 and kt == 8:
                            turn_att(s_, b - 1)
                        if ahead and kt == 9:
                            max_rows(s_, n + 2, s2)
                        if before and s == 0 and kt == 11:
                            project(s_, b - 1)
                        if kt >= LAG:
                            values(s_, b, s, kt - LAG)
                        elif before:
                            values(s_, b if s else b - 1, (s - 1) % SLOTS, KT + kt - LAG)

            def finish(s_, b):
                for kt in range(KT - LAG, KT):
                    pe.wait_ge(s_.exp_done, EXP0 + SLOTS * KT * (b + 1) - KT + kt + 1)
                    values(s_, b, SLOTS - 1, kt)
                turn_o(s_, b, SLOTS * (b + 1) - 1, SLOTS - 1)
                turn_att(s_, b)
                project(s_, b)

            pe.wait_ge(qf_done, 2 * NTG)
            pe.wait_ge(xt_done, KC * NTG)
            pe.wait_ge(v_done, V0 + KT * B)
            def prepare(s_, b):
                for s in range(2):
                    for h in range(HG):
                        maxima_of(s_, SLOTS * b + s, b, s, h)
                    max_rows(s_, SLOTS * b + s, s)

            prepare(first, 0)
            pe.wait_ge(o_zeroed, 1)
            attention(first, 0, True, False)
            with pe.Fori(1, B - 1) as b:
                attention(first, b, False, False)
            attention(first, B - 1, False, True)
            finish(first, B - 1)
            pe.wait_ge(first.max_taken, ONE + first.uses * SLOTS * B)
            pe.wait_ge(good_steps, SLOTS * B + 2)
            nc.tensor.matmul(MB[0:1, 0:P], good_p[:], idn[:], start=True, stop=True).then_inc(good_ready, 1)
            with failed(pe):
                with pe.Fori(0, B) as b:
                    prepare(whole, b)
                    attention(whole, b, True, True)
                    finish(whole, b)
                pe.wait_ge(whole.max_taken, ONE + whole.uses * SLOTS * B)
                pe.wait_ge(whole.x_taken, ONE + XU * B)

            pe.wait_ge(mlpw_lo, 2)
            pe.wait_ge(first.x_taken, ONE + XU * B)
            pe.wait_ge(flag_done, 1)
            turn((MB[:, :], XB[:, :]), yn, 0, yn_done, yt_done, yt_ready)
            for c in range(NTG):
                pe.wait_ge(ylo_done, c + 1)
                for i in range(NI):
                    j = NI * c + i
                    if j >= 4:
                        pe.wait_ge(g_done, j - 3)
                    cut = slice(i * P, (i + 1) * P)
                    product3(S[:, j % 4, :], [(fc_hi[:, k, cut], fc_lo[:, k, cut]) for k in range(KC)],
                             [(y_hi[:, c % 2, k, :], y_lo[:, c % 2, k, :]) for k in range(KC)]).then_inc(fc_ready, 1)
                    if i == 3 and c + 1 < NTG:
                        turn((MB[:, :], XB[:, :]), yn, c + 1, yn_done, yt_done, yt_ready)
                for t in range(TT):
                    n = TT * c + t
                    if n >= 2:
                        pe.wait_ge(ob_half, n - 1)
                    for i in range(NI):
                        if t == 0:
                            pe.wait_ge(glo_done, NI * c + i + 1)
                        cut = slice(t * P, (t + 1) * P)
                        for m, (w, v) in enumerate(((g_hi, pj_hi), (g_hi, pj_lo), (g_lo, pj_hi))):
                            last = nc.tensor.matmul(O[:, n % 2, 0:D], w[:, i, cut], v[:, i, :],
                                                    start=i == 0 and m == 0, stop=i == NI - 1 and m == 2)
                    last.then_inc(pj_ready, 1)


def kernel(x, ctx_2048, mask_BxS2_bf1, **w):
    import concourse.bacc as bacc
    from concourse.bass_utils import run_bass_kernel_spmd

    w = {n.removeprefix("L0_xattn_"): np.asarray(a) for n, a in w.items()}
    con = np.ascontiguousarray

    def chunks(a):
        return a.reshape(-1, P, a.shape[-1]).transpose(1, 0, 2)

    def by_width(a):
        return a.reshape(*a.shape[:-1], 2, HM, HD).swapaxes(-1, -2).reshape(a.shape)

    def column(a):
        return a.reshape(-1, P).T

    arrays = {
        "x": con(np.asarray(x).reshape(TOK, P, D)),
        "ctx_t": con(np.asarray(ctx_2048).transpose(0, 2, 1).reshape(B, KC, P, LK)),
        "mask": con(np.asarray(mask_BxS2_bf1)).view(np.uint8),
        "w_kv": con(np.stack([chunks(by_width(w["k_w"])), chunks(w["v_w"])], 1)),
        "w_qc": con(np.stack([chunks(by_width(w["q_w"])), chunks(w["cproj_w"])], 1)),
        "fc": con(chunks(w["fc_w"])),
        "pj": con(chunks(w["proj_w"])),
        "cols": con(np.concatenate([column(a) for a in (
            w["ln1_w"], w["ln1_b"], w["ln2_w"], w["ln2_b"], by_width(w["q_b"]), by_width(w["k_b"]), w["fc_b"])], 1)),
        "rows": con(np.stack([w["v_b"], w["cproj_b"], w["proj_b"]])),
        "ident": np.eye(P, dtype=np.float32),
    }
    nc = bacc.Bacc("TRN2", target_bir_lowering=False, num_devices=1)
    aps = {n: nc.dram_tensor(f"in_{n}", a.shape, mybir.dt.from_np(a.dtype), kind="ExternalInput").ap()
           for n, a in arrays.items()}
    out = nc.dram_tensor("out", [B * LQ, D], F32, kind="ExternalOutput").ap()
    build(nc, out=out, **aps)
    r = run_bass_kernel_spmd(nc, [{f"in_{n}": a for n, a in arrays.items()}], core_ids=[0])
    return r.results[0]["out"].reshape(B, LQ, D)
```

```python
from contextlib import ExitStack

import numpy as np

import concourse.bass as bass
from concourse import mybir

F32 = mybir.dt.float32
F32R = mybir.dt.float32r
BF16 = mybir.dt.bfloat16
U8 = mybir.dt.uint8
I32 = mybir.dt.int32
ALU = mybir.AluOpType
ACT = mybir.ActivationFunctionType
AX = mybir.AxisListType

P = 128
B, LQ, LK, D = 8, 256, 1601, 256
H, HD = 16, 16
INNER = 4 * D
KC = D // P
TOK = B * LQ // P
QT = LQ // P
KT = -(-LK // P)
KP = KT * P
TAIL = LK - (KT - 1) * P
HG = 4
SLOTS = H // HG
HM = P // HD
VW = HD + 1
NT = [3, 3, 3, 4]
CH = len(NT)
T0 = [sum(NT[:c]) for c in range(CH)]
NK = [min(LK, (T0[c] + NT[c]) * P) - T0[c] * P for c in range(CH)]
NKE = [n + n % 2 for n in NK]
NKM = max(NKE)
QSTACK = ((0, 3), (3, 2), (5, 1))
ROWS = 6 * HD
MASKROW, MAXROW = ROWS, ROWS + 1
KROWS = ROWS + 4
SCALE = 1.0 / float(np.sqrt(HD))
EPS = 1e-5
MASKED = 1e30
LARGE = 1e30
TG = 512
NTG = B * LQ // TG
TT = TG // P
NI = INNER // P
QG = HG * LQ
PBUF = 4
LAG = 2
MAXSTEPS = [1, 3, 5, 7]
OPENSTEPS = [5, 6, 7, 9]

class Section:
    pass


BLOCKKEYS = [[(q * 256, q, 0, 256) for q in range(QT)]]
ALLKEYS = [[(0, q, k, min(401, LK - k))] for q in range(QT) for k in range(0, LK, 401)]


def build(nc, x, ctx_t, mask, w_kv, w_qc, fc, pj, cols, rows, ident, out):
    stack = ExitStack()
    with stack:
        def sb(name, shape, dt, where=stack):
            return where.enter_context(nc.sbuf_tensor(name, shape, dt))

        def sem(name):
            return stack.enter_context(nc.semaphore(name))

        k_scr = nc.dram_tensor("k_scr", [B, 2, 3, P, KP], BF16).ap()
        v_scr = nc.dram_tensor("v_scr", [B, SLOTS, P, KT * HG * VW], F32).ap()
        q_scr = nc.dram_tensor("q_scr", [B, 2, 3, P, LQ], BF16).ap()
        mask_scr = nc.dram_tensor("mask_scr", [B, LK], BF16).ap()
        some_scr = nc.dram_tensor("some_scr", [1, B], F32).ap()

        S = stack.enter_context(nc.psum_tensor("S", [P, 4, 512], F32))
        O = stack.enter_context(nc.psum_tensor("O", [P, 2, 512], F32))
        MB = stack.enter_context(nc.psum_tensor("MB", [P, 512], F32))
        XB = stack.enter_context(nc.psum_tensor("XB", [P, 512], F32))

        idn = sb("idn", [P, P], F32)
        xs = sb("xs", [P, TOK, D], F32)
        good = sb("good", [P, QT, HG], F32)
        good_p = sb("good_p", [P, 1], F32)
        good_all = sb("good_all", [1, 1], F32)
        flag = sb("flag", [1, 1], I32)
        hid = sb("hid", [P, TOK, D], F32)
        st = sb("st", [P, TOK, 6], F32)
        mv2 = sb("mv2", [P, TOK, 2], F32)
        rs = sb("rs", [P, 4, TOK], F32)
        cols_s = sb("cols_s", [P, 20], F32)
        rows_s = sb("rows_s", [P, 3, D], F32)
        w_qc_s = sb("w_qc_s", [P, 2, KC, D], F32)
        some = sb("some", [P, B], F32)
        mx = sb("mx", [P, 2, QT, HG], F32)
        mres = sb("mres", [HG, LQ], F32)
        mrow = sb("mrow", [HG, 2, 3, LQ], BF16)
        ln1_w, ln1_b, ln2_w, ln2_b = (cols_s[:, 2 * i:2 * i + 2] for i in range(4))
        bq_s, bk_s, fcb_s = cols_s[:, 8:10], cols_s[:, 10:12], cols_s[:, 12:20]
        bv_s, bc_s, pjb_s = (rows_s[:, i, :] for i in range(3))

        mid = ExitStack()
        kst = sb("kst", [P, SLOTS, HG, KP], BF16, mid)
        qst = sb("qst", [P, SLOTS, HG, LQ], BF16, mid)
        vsl = sb("vsl", [P, SLOTS, KT, HG * VW], F32, mid)

        early = ExitStack()
        w_raw = sb("w_raw", [P, 2, KC, D], F32, early)
        w_hi = sb("w_hi", [P, 2, KC, D], F32R, early)
        w_lo = sb("w_lo", [P, 2, KC, D], F32R, early)
        cT = sb("cT", [P, CH, KC, NKM], F32, early)
        c_hi = sb("c_hi", [P, CH, KC, NKM], F32R, early)
        c_lo = sb("c_lo", [P, CH, KC, NKM], F32R, early)
        kpart = sb("kpart", [P, 2, 2, 3, NKM], BF16, early)
        kres = sb("kres", [P, 2, NKM], F32, early)
        vst = sb("vst", [P, 2, SLOTS, max(NT), HG * VW], F32, early)
        ones = sb("ones", [3, KP], BF16, early)
        mk_u = sb("mk_u", [B, LK], U8, early)
        mk_room = hid[0:B, 2 * QT:TOK - QT, :].rearrange("p t d -> p (t d)")
        mk_f = mk_room[:, 0:LK]
        mk_b = mk_room[:, LK:LK + LK // 2 + 1].bitcast(BF16)[:, 0:LK]
        some_b = sb("some_b", [B, 2], F32, early)
        xst = sb("xst", [P, QT, 6], F32, early)
        xmv = sb("xmv", [P, QT, 2], F32, early)
        xrs = sb("xrs", [P, 4, QT], F32, early)
        qf = hid[:, TOK - QT:TOK, :]
        qres = sb("qres", [P, 2, LQ], F32, early)
        qpart = sb("qpart", [P, 2, 3, LQ], BF16, early)
        early.close()
        xn = hid[:, 0:QT, :]
        xT = hid[:, QT:2 * QT, :]

        late = ExitStack()
        pr = sb("pr", [P, PBUF, QG], F32, late)
        mxp = sb("mxp", [P, QT, HG, 4], F32, late)
        osb = sb("osb", [P, 2, LQ], F32, late)
        rec = sb("rec", [P, QT, HG], F32, late)
        att = sb("att", [P, QT, D], F32, late)
        attT = sb("attT", [P, KC, LQ], F32, late)
        fc_raw = sb("fc_raw", [P, KC, INNER], F32, late)
        pj_raw = sb("pj_raw", [P, NI, D], F32, late)
        fc_hi = sb("fc_hi", [P, KC, INNER], F32R, late)
        fc_lo = sb("fc_lo", [P, KC, INNER], F32R, late)
        pj_hi = sb("pj_hi", [P, NI, D], F32R, late)
        pj_lo = sb("pj_lo", [P, NI, D], F32R, late)
        late.close()
        yn = fc_raw[:].rearrange("p k (a d) -> p (k a) d", d=D).rearrange("p (a t) d -> p a t d", a=2)
        yT = pj_raw[:].rearrange("p (a k u) d -> p a k (u d)", a=2, k=KC)

        mid.close()
        last = ExitStack()
        y_hi = sb("y_hi", [P, 2, KC, TG], F32R, last)
        y_lo = sb("y_lo", [P, 2, KC, TG], F32R, last)
        g = sb("g", [P, 2, TG], F32, last)
        g_hi = sb("g_hi", [P, NI, TG], F32R, last)
        g_lo = sb("g_lo", [P, NI, TG], F32R, last)
        ob = sb("ob", [P, 2, D], F32, last)
        last.close()

        cols_in, rows_in, wkv_in, wqc_in, idn_in, x_in, xrest_in, mask_in = map(
            sem, ("cols_in", "rows_in", "wkv_in", "wqc_in", "idn_in", "x_in", "xrest_in", "mask_in"))
        ctx_in = [sem(f"ctx_in{c}") for c in range(CH)]
        k_out = [sem(f"k_out{i}") for i in range(2)]
        v_out = [sem(f"v_out{i}") for i in range(2)]
        q_out = sem("q_out")
        out_done = [sem(f"out_done{i}") for i in range(2)]
        mask_out, some_out, some_in, ones_in, mlpw_in = map(
            sem, ("mask_out", "some_out", "some_in", "ones_in", "mlpw_in"))
        pads_set, w_split, mask_steps = map(sem, ("pads_set", "w_split", "mask_steps"))
        hi_done, lo_done = sem("hi_done"), sem("lo_done")
        k_ready, kh_done, kres_done, km_done, kl_done = map(
            sem, ("k_ready", "kh_done", "kres_done", "km_done", "kl_done"))
        v_ready, v_done = sem("v_ready"), sem("v_done")
        ln_steps, root_done = sem("ln_steps"), sem("root_done")
        good_steps, good_ready, flag_done = map(sem, ("good_steps", "good_ready", "flag_done"))
        xn_done, xt_ready, xt_done, xb_done = map(sem, ("xn_done", "xt_ready", "xt_done", "xb_done"))
        q_ready, qf_done, qh_done, qres_done, qm_done, ql_done = map(
            sem, ("q_ready", "qf_done", "qh_done", "qres_done", "qm_done", "ql_done"))
        o_zeroed = sem("o_zeroed")
        mlpw_hi, mlpw_lo = sem("mlpw_hi"), sem("mlpw_lo")
        yn_done, yt_ready, yt_done, yhi_done, ylo_done = map(
            sem, ("yn_done", "yt_ready", "yt_done", "yhi_done", "ylo_done"))
        fc_ready, g_done, ghi_done, glo_done, pj_ready, ob_half, ob_done = map(
            sem, ("fc_ready", "g_done", "ghi_done", "glo_done", "pj_ready", "ob_half", "ob_done"))
        KRES0 = 4
        V0 = 4
        KL0 = OUT0 = 1
        QF0 = 1
        EXP0 = 2
        O0 = 2
        ONE = 1

        def section(name, maxima):
            s = Section()
            s.maxima = maxima
            s.uses = HG * len(maxima) + 1
            s.slot_in = [sem(f"{name}_slot_in{i}") for i in range(SLOTS)]
            s.mrow_in = [sem(f"{name}_mrow_in{i}") for i in range(SLOTS)]
            s.scores_done = sem(f"{name}_scores_done")
            s.exp_done = sem(f"{name}_exp_done")
            s.o_ready = sem(f"{name}_o_ready")
            s.o_taken = sem(f"{name}_o_taken")
            s.max_ready = sem(f"{name}_max_ready")
            s.max_taken = sem(f"{name}_max_taken")
            s.mx_done = sem(f"{name}_mx_done")
            s.m_steps = sem(f"{name}_m_steps")
            s.mrow_done = sem(f"{name}_mrow_done")
            s.x_ready = sem(f"{name}_x_ready")
            s.x_taken = sem(f"{name}_x_taken")
            s.rec_done = sem(f"{name}_rec_done")
            s.h_steps = sem(f"{name}_h_steps")
            s.var_done = sem(f"{name}_var_done")
            s.root_done = sem(f"{name}_root_done")
            s.rstd_steps = sem(f"{name}_rstd_steps")
            s.yn0_done = sem(f"{name}_yn0_done")
            return s

        XU = SLOTS + 2
        LNVAR = 2 * QT + 1
        LNSTEPS = LNVAR + 5
        HEAD = TOK - QT
        first = section("first", BLOCKKEYS)
        whole = section("whole", ALLKEYS)

        def failed(eng):
            eng.wait_ge(flag_done, 1)
            return eng.If(eng.value_load(flag[0:1, 0:1], min_val=0, max_val=1) < 1)

        block = stack.enter_context(nc.Block())

        def v_bank(kt):
            return (O[:, 0, :], O[:, 1, :], MB[:, :], XB[:, :])[kt % 4]

        def load_ctx(eng, b, c):
            eng.dma_start(cT[:, c, :, 0:NK[c]], ctx_t[bass.ds(b, 1), :, :, T0[c] * P:T0[c] * P + NK[c]]
                          .rearrange("o k p t -> p (o k) t")).then_inc(ctx_in[c], 16)

        @block.sync
        def _(sp):
            def store_kv(b, c):
                i, t, n = c % 2, T0[c] * P, NK[c]
                sp.wait_ge(kl_done, KL0 + 2 * (CH * b + c + 1))
                for mt in range(2):
                    sp.dma_start(k_scr[bass.ds(b, 1), mt, :, :, t:t + n].rearrange("o r p t -> p (o r) t"),
                                 kpart[:, i, mt, :, 0:n]).then_inc(k_out[i], 16)
                sp.wait_ge(v_done, V0 + KT * b + T0[c] + NT[c])
                sp.dma_start(v_scr[bass.ds(b, 1), :, :, T0[c] * HG * VW:(T0[c] + NT[c]) * HG * VW]
                             .rearrange("o s p w -> p (o s) w"),
                             vst[:, i, :, 0:NT[c], :].rearrange("p s t w -> p s (t w)")).then_inc(v_out[i], 16)

            sp.sem_inc(q_out, OUT0)
            for i in range(2):
                sp.sem_inc(k_out[i], OUT0)
                sp.sem_inc(v_out[i], OUT0)
            for s_ in (first, whole):
                for s in range(SLOTS):
                    sp.sem_inc(s_.mrow_in[s], ONE)
            sp.dma_start(w_raw[:], w_kv).then_inc(wkv_in, 16)
            load_ctx(sp, 0, 0)
            load_ctx(sp, 0, 1)
            sp.dma_start(xs[:, 0:QT, :], x[0:QT].rearrange("n p d -> p n d")).then_inc(x_in, 16)
            load_ctx(sp, 0, 2)
            sp.dma_start(w_qc_s[:], w_qc).then_inc(wqc_in, 16)
            load_ctx(sp, 0, 3)
            sp.wait_ge(mask_steps, 4)
            sp.dma_start(mask_scr, mk_b).then_inc(mask_out, 16)
            sp.dma_start(some_scr.rearrange("o b -> b o"), some_b[:, 1:2]).then_inc(some_out, 16)
            sp.wait_ge(some_out, 16)
            sp.dma_start(some[:], some_scr[0].partition_broadcast(P)).then_inc(some_in, 16)
            sp.wait_ge(pads_set, 5)
            sp.dma_start(kst[MAXROW:MAXROW + 3, :, :, :].rearrange("p s h t -> p (s h) t"),
                         ones[:].unsqueeze(1).broadcast_to([3, H, KP])).then_inc(ones_in, 16)
            sp.dma_start(qst[MASKROW:MASKROW + 1, :, :, :].rearrange("p s h t -> p (s h) t"),
                         ones[0:1, 0:LQ].unsqueeze(1).broadcast_to([1, H, LQ])).then_inc(ones_in, 16)
            sp.dma_start(xs[:, QT:TOK, :], x[QT:TOK].rearrange("n p d -> p n d")).then_inc(xrest_in, 16)

            def store_q(b):
                for mt in range(2):
                    sp.wait_ge(ql_done, 2 * b + mt + 1)
                    sp.dma_start(q_scr[bass.ds(b, 1), mt].rearrange("o r p q -> p (o r) q"),
                                 qpart[:, mt, :, :]).then_inc(q_out, 16)

            def all_out(batches):
                for i in range(2):
                    sp.wait_ge(k_out[i], OUT0 + 16 * 2 * batches * CH // 2)
                    sp.wait_ge(v_out[i], OUT0 + 16 * batches * CH // 2)
                sp.wait_ge(q_out, OUT0 + 16 * 2 * batches)

            with sp.Fori(0, B - 2) as b:
                for c in range(CH):
                    store_kv(b, c)
                store_q(b)

            def fill(s_, b, s, quarters=range(4)):
                rows_of = k_scr[bass.ds(b, 1), s // 2].rearrange("o r (d h) t -> (o r d) h t", h=HM)[
                    :, HG * (s % 2):HG * (s % 2) + HG, 0:LK]

                def fill_k(r0, parts):
                    sp.dma_start(kst[r0:r0 + parts * HD, s, :, 0:LK], rows_of[0:parts * HD]
                                 ).then_inc(s_.slot_in[s], 16)

                if 0 in quarters:
                    fill_k(0, 3)
                if 1 in quarters:
                    fill_k(3 * HD, 2)
                    fill_k(5 * HD, 1)
                if 2 in quarters:
                    sp.dma_start(kst[MASKROW:MASKROW + 1, s, :, 0:LK],
                                 mask_scr[bass.ds(b, 1), :].unsqueeze(1).broadcast_to([1, HG, LK])
                                 ).then_inc(s_.slot_in[s], 16)
                    sp.dma_start(vsl[:, s, :, :].rearrange("p t w -> p (t w)"),
                                 v_scr[bass.ds(b, 1), s].rearrange("o p w -> (o p) w")).then_inc(s_.slot_in[s], 16)
                if 3 in quarters:
                    for part, (g0, ng) in enumerate(QSTACK):
                        sp.dma_start(qst[g0 * HD:(g0 + ng) * HD, s, :, :].rearrange("p h q -> p (h q)"),
                                     q_scr[bass.ds(b, 1), s // 2, part].rearrange("o (d h) q -> o d (h q)", h=HM)[
                                         :, :, QG * (s % 2):QG * (s % 2) + QG].broadcast_to([ng, HD, QG])
                                     ).then_inc(s_.slot_in[s], 16)

            def send_rows(s_, b, s):
                sp.wait_ge(s_.mrow_done, SLOTS * b + s + 1)
                for part in range(3):
                    r = MAXROW + part
                    sp.dma_start(qst[r:r + 1, s, :, :], mrow[:, s % 2, part, :]).then_inc(s_.mrow_in[s], 16)

            QUARTERS = [[0], [1], [2, 3], []]
            all_out(B - 2)
            sp.wait_ge(mask_out, 16)
            sp.wait_ge(ones_in, 32)
            for c in range(CH):
                store_kv(B - 2, c)
                fill(first, 0, 0, QUARTERS[c])
            store_q(B - 2)
            for c in range(CH):
                if c == 2:
                    send_rows(first, 0, 0)
                store_kv(B - 1, c)
                fill(first, 0, 1, QUARTERS[c])

            def attention(s_, b, start, final):
                for s in range(SLOTS):
                    if s == 0 or not final:
                        sp.wait_ge(s_.o_ready, ONE + SLOTS * b + s)
                        fill(s_, b if s == 0 else b + 1, (s + 3) % SLOTS)
                    if start and s == 0:
                        send_rows(s_, b, 1)
                    if s < 2 or not final:
                        send_rows(s_, b if s < 2 else b + 1, (s + 2) % SLOTS)

            store_q(B - 1)
            fill(first, 0, 2)
            all_out(B)
            attention(first, 0, True, False)
            sp.dma_start(fc_raw[:], fc).then_inc(mlpw_in, 16)
            sp.dma_start(pj_raw[:], pj).then_inc(mlpw_in, 16)
            with sp.Fori(1, B - 1) as b:
                attention(first, b, False, False)
            attention(first, B - 1, False, True)
            with failed(sp):
                with sp.Fori(0, B) as b:
                    sp.wait_ge(whole.o_ready, ONE + SLOTS * b)
                    for s in range(SLOTS - 1):
                        fill(whole, b, s)
                    send_rows(whole, b, 0)
                    attention(whole, b, True, True)

            for t in range(TOK):
                sp.wait_ge(ob_done, t + 1)
                sp.dma_start(out[t * P:(t + 1) * P, :], ob[:, t % 2, :]).then_inc(out_done[t % 2], 16)
            for i in range(2):
                sp.wait_ge(out_done[i], 16 * TOK // 2)

        @block.gpsimd
        def _(pool):
            nc.gpsimd.memset(ones[:], 1.0).then_inc(pads_set, 1)
            nc.gpsimd.memset(cT[:, CH - 1, :, NK[-1]:NKM], 0.0).then_inc(pads_set, 1)
            nc.gpsimd.memset(vst[:], 1.0).then_inc(pads_set, 1)
            pool.wait_ge(pads_set, 3)
            nc.gpsimd.memset(vst[64:P, 1, :, NT[-1] - 1, :], 0.0).then_inc(pads_set, 1)
            pool.wait_ge(pads_set, 4)
            nc.gpsimd.memset(kst[:, :, :, LK:KP], 0.0).then_inc(pads_set, 1)
            pool.wait_ge(pads_set, 5)
            nc.gpsimd.memset(vst[64:TAIL, 1, :, NT[-1] - 1, :], 1.0).then_inc(pads_set, 1)

            def c_low(b, c):
                pool.wait_ge(hi_done, CH * b + c + 1)
                n = NKE[c]
                nc.gpsimd.tensor_tensor(c_lo[:, c, :, 0:n], cT[:, c, :, 0:n], c_hi[:, c, :, 0:n].bitcast(F32),
                                        ALU.subtract).then_inc(lo_done, 1)

            def k_low(b, c):
                i, n = c % 2, NK[c]
                for mt in range(2):
                    pool.wait_ge(km_done, 2 * (CH * b + c) + mt + 1)
                    nc.gpsimd.tensor_tensor(kpart[:, i, mt, 2, 0:n], kres[:, mt, 0:n], kpart[:, i, mt, 1, 0:n],
                                            ALU.subtract).then_inc(kl_done, 1)

            c_low(0, 0)
            c_low(0, 1)
            with pool.Fori(0, B - 1) as b:
                for c in range(CH):
                    c_low(b if c < 2 else b + 1, (c + 2) % CH)
                    k_low(b, c)
            for c in range(CH):
                if c < 2:
                    c_low(B - 1, c + 2)
                k_low(B - 1, c)
            pool.wait_ge(rows_in, 16)
            pool.wait_ge(xn_done, B)
            nc.gpsimd.tensor_tensor(xs[:], xs[:], bc_s.unsqueeze(1).broadcast_to([P, TOK, D]),
                                    ALU.add).then_inc(xb_done, 1)

            pool.wait_ge(mlpw_in, 32)
            nc.gpsimd.tensor_copy(fc_hi[:], fc_raw[:]).then_inc(mlpw_hi, 1)
            nc.gpsimd.tensor_copy(pj_hi[:], pj_raw[:]).then_inc(mlpw_hi, 1)
            pool.wait_ge(mlpw_hi, 2)
            nc.gpsimd.tensor_tensor(fc_lo[:], fc_raw[:], fc_hi[:].bitcast(F32), ALU.subtract).then_inc(mlpw_lo, 1)
            nc.gpsimd.tensor_tensor(pj_lo[:], pj_raw[:], pj_hi[:].bitcast(F32), ALU.subtract).then_inc(mlpw_lo, 1)
            for c in range(NTG):
                pool.wait_ge(yhi_done, c + 1)
                if c >= 2:
                    pool.wait_ge(fc_ready, NI * (c - 1))
                nc.gpsimd.tensor_tensor(y_lo[:, c % 2], yT[:, c % 2], y_hi[:, c % 2].bitcast(F32),
                                        ALU.subtract).then_inc(ylo_done, 1)

        @block.scalar
        def _(act):
            act.dma_start(mk_u[:], mask).then_inc(mask_in, 16)
            act.dma_start(cols_s[:], cols).then_inc(cols_in, 16)
            act.dma_start(rows_s[:], rows.partition_broadcast(P)).then_inc(rows_in, 16)
            act.dma_start(idn[:], ident).then_inc(idn_in, 16)

            def high(b, c):
                act.wait_ge(ctx_in[c], 16 * (b + 1))
                if not isinstance(b, int) or b > 0:
                    act.wait_ge(v_ready, KT * (b - 1) + T0[c] + NT[c])
                nc.scalar.activation(c_hi[:, c, :, 0:NKE[c]], cT[:, c, :, 0:NKE[c]], ACT.Copy
                                     ).then_inc(hi_done, 1)

            def k_parts(b, c, load):
                i, n = c % 2, NK[c]
                if c == CH - 1:
                    x_t(b)
                act.wait_ge(k_out[i], OUT0 + 16 * 2 * (2 * b + c // 2))
                for mt in range(2):
                    j = 2 * c + mt
                    act.wait_ge(k_ready, 2 * CH * b + j + 1)
                    nc.scalar.activation(kpart[:, i, mt, 0, 0:n], S[:, j % 4, 0:n], ACT.Identity,
                                         bias=bk_s[:, mt:mt + 1]).then_inc(kh_done, 1)
                    if mt == 0 and load:
                        load_ctx(act, *load)
                for mt in range(2):
                    act.wait_ge(kres_done, KRES0 + 2 * (CH * b + c) + mt + 1)
                    nc.scalar.activation(kpart[:, i, mt, 1, 0:n], kres[:, mt, 0:n], ACT.Copy).then_inc(km_done, 1)

            def x_t(b):
                act.wait_ge(xt_ready, b + 1)
                for k in range(KC):
                    nc.scalar.activation(xT[:, k, :], S[:, 0, k * LQ:(k + 1) * LQ], ACT.Identity,
                                         bias=ln1_b[:, k:k + 1], scale=ln1_w[:, k:k + 1]).then_inc(xt_done, 1)

            def q_parts(b):
                act.wait_ge(q_out, OUT0 + 16 * 2 * b)
                for mt in range(2):
                    act.wait_ge(qf_done, QF0 + 2 * b + mt + 1)
                    nc.scalar.activation(qpart[:, mt, 0, :], qf[:, mt, :], ACT.Copy).then_inc(qh_done, 1)
                for mt in range(2):
                    act.wait_ge(qres_done, 2 * b + mt + 1)
                    nc.scalar.activation(qpart[:, mt, 1, :], qres[:, mt, :], ACT.Copy).then_inc(qm_done, 1)

            def x_root(b):
                act.wait_ge(ln_steps, LNSTEPS * b + LNVAR)
                nc.scalar.activation(xrs[:, 1, :], xrs[:, 0, :], ACT.Sqrt).then_inc(root_done, 1)

            act.wait_ge(cols_in, 16)
            act.wait_ge(pads_set, 6)
            for c in range(2):
                high(0, c)
            x_root(0)
            for c in range(2):
                high(0, c + 2)
                k_parts(0, c, (1, c))
            with act.Fori(0, B - 2) as b:
                x_root(b + 1)
                for c in range(2):
                    high(b + 1, c)
                    k_parts(b, c + 2, (b + 1, c + 2))
                q_parts(b)
                for c in range(2):
                    high(b + 1, c + 2)
                    k_parts(b + 1, c, (b + 2, c))
            x_root(B - 1)
            for c in range(2):
                high(B - 1, c)
                k_parts(B - 2, c + 2, (B - 1, c + 2))
            q_parts(B - 2)
            for c in range(2):
                high(B - 1, c + 2)
                k_parts(B - 1, c, None)
            for c in range(2):
                k_parts(B - 1, c + 2, None)
            q_parts(B - 1)

            assert PBUF >= LAG + 2 and (SLOTS * KT) % PBUF == 0 and (SLOTS * KT) % 2 == 0

            def attention(s_, b):
                for n in range(SLOTS * KT):
                    act.wait_ge(s_.scores_done, SLOTS * KT * b + n + 1)
                    nc.scalar.activation(pr[:, n % PBUF, :], S[:, 2 * (n % 2):2 * (n % 2) + 2, :]
                                         .rearrange("p a n -> p (a n)"), ACT.Exp).then_inc(s_.exp_done, 1)

            def root(s_, i, t0, t1):
                act.wait_ge(s_.var_done, i + 1)
                nc.scalar.activation(rs[:, 1, t0:t1], rs[:, 0, t0:t1], ACT.Sqrt).then_inc(s_.root_done, 1)

            act.sem_inc(first.exp_done, EXP0)
            act.sem_inc(whole.exp_done, EXP0)
            with act.Fori(0, B) as b:
                attention(first, b)
            root(first, 0, 0, TOK - QT)
            root(first, 1, TOK - QT, TOK)
            with failed(act):
                with act.Fori(0, B) as b:
                    attention(whole, b)
                root(whole, 0, 0, TOK)


            def y_t(c):
                for k in range(KC):
                    act.wait_ge(yt_ready, KC * c + k + 1)
                    if c >= 2:
                        act.wait_ge(ylo_done, c - 1)
                    nc.scalar.activation(yT[:, c % 2, k, :], (MB, XB)[k][:, :], ACT.Identity,
                                         bias=ln2_b[:, k:k + 1], scale=ln2_w[:, k:k + 1]).then_inc(yt_done, 1)

            act.wait_ge(mlpw_lo, 2)
            y_t(0)
            for c in range(NTG):
                for i in range(NI):
                    j = NI * c + i
                    act.wait_ge(fc_ready, j + 1)
                    if j >= 2:
                        act.wait_ge(glo_done, j - 1)
                    nc.scalar.activation(g[:, j % 2, :], S[:, j % 4, :], ACT.Gelu_apprx_tanh,
                                         bias=fcb_s[:, i:i + 1]).then_inc(g_done, 1)
                    if i == 4 and c + 1 < NTG:
                        y_t(c + 1)

        @block.vector
        def _(dve):
            dve.sem_inc(kres_done, KRES0)
            dve.sem_inc(kl_done, KL0)
            dve.sem_inc(v_done, V0)
            dve.sem_inc(qf_done, QF0)
            for s_ in (first, whole):
                dve.sem_inc(s_.o_taken, O0)
                dve.sem_inc(s_.max_taken, ONE)
                dve.sem_inc(s_.x_taken, ONE)
            dve.wait_ge(wkv_in, 16)
            nc.vector.tensor_copy(w_hi[:], w_raw[:]).then_inc(w_split, 1)
            dve.wait_ge(w_split, 1)
            nc.vector.tensor_tensor(w_lo[:], w_raw[:], w_hi[:].bitcast(F32), ALU.subtract).then_inc(w_split, 1)
            dve.wait_ge(mask_in, 16)
            nc.vector.tensor_copy(mk_f, mk_u[:]).then_inc(mask_steps, 1)
            dve.wait_ge(mask_steps, 1)
            nc.vector.tensor_reduce(some_b[:, 0:1], mk_f, AX.X, ALU.max).then_inc(mask_steps, 1)
            dve.wait_ge(mask_steps, 2)
            nc.vector.tensor_scalar(mk_b, mk_f, some_b[:, 0:1], MASKED, ALU.subtract, ALU.mult
                                    ).then_inc(mask_steps, 1)
            nc.vector.tensor_scalar(some_b[:, 1:2], some_b[:, 0:1], SCALE, None, ALU.mult).then_inc(mask_steps, 1)

            def k_rest(b, c):
                i, n = c % 2, NK[c]
                dve.wait_ge(kl_done, KL0 + 2 * (CH * b + c))
                for mt in range(2):
                    j = 2 * c + mt
                    dve.wait_ge(kh_done, 2 * CH * b + j + 1)
                    nc.vector.scalar_tensor_tensor(out=kres[:, mt, 0:n], in0=S[:, j % 4, 0:n],
                                                   scalar=bk_s[:, mt:mt + 1], in1=kpart[:, i, mt, 0, 0:n],
                                                   op0=ALU.add, op1=ALU.subtract).then_inc(kres_done, 1)

            def v_tiles(b, c, final):
                dve.wait_ge(v_out[c % 2], OUT0 + 16 * (2 * b + c // 2))
                for t in range(NT[c]):
                    kt = T0[c] + t
                    m = TAIL if kt == KT - 1 else P
                    dve.wait_ge(v_ready, KT * b + kt + 1)
                    nc.vector.tensor_tensor(
                        vst[0:m, c % 2, :, t, :].rearrange("p s (h w) -> p s h w", w=VW)[:, :, :, 0:HD],
                        v_bank(kt)[0:m, 0:D].rearrange("p (s h d) -> p s h d", s=SLOTS, d=HD),
                        bv_s[0:m, :].rearrange("p (s h d) -> p s h d", s=SLOTS, d=HD), ALU.add).then_inc(v_done, 1)
                    if c == CH - 1 and t == 0:
                        q_full(b)
                    if final and c == 1 and t >= 1:
                        maxima_of(first, 0, 0, t + 1)

            def newton(rs_, steps, before, root, roots):
                dve.wait_ge(root, roots)
                nc.vector.reciprocal(rs_[2], rs_[1]).then_inc(steps, 1)
                dve.wait_ge(steps, before + 1)
                nc.vector.tensor_tensor(rs_[3], rs_[0], rs_[2], ALU.mult).then_inc(steps, 1)
                dve.wait_ge(steps, before + 2)
                nc.vector.tensor_tensor(rs_[3], rs_[3], rs_[2], ALU.mult).then_inc(steps, 1)
                dve.wait_ge(steps, before + 3)
                nc.vector.tensor_scalar(rs_[3], rs_[3], -0.5, 1.5, ALU.mult, ALU.add).then_inc(steps, 1)
                dve.wait_ge(steps, before + 4)
                nc.vector.tensor_tensor(rs_[2], rs_[2], rs_[3], ALU.mult).then_inc(steps, 1)
                dve.wait_ge(steps, before + 5)

            def x_sums(b):
                dve.wait_ge(x_in if isinstance(b, int) and b == 0 else xrest_in, 16)
                for q in range(QT):
                    nc.vector.bn_stats(xst[:, q, :], xs[:, bass.ds(QT * b + q, 1), :]).then_inc(ln_steps, 1)

            def x_moments(b):
                for q in range(QT):
                    nc.vector.bn_aggr(xmv[:, q, :], xst[:, q, :]).then_inc(ln_steps, 1)
                dve.wait_ge(ln_steps, LNSTEPS * b + 2 * QT)
                nc.vector.tensor_scalar(xrs[:, 0, :], xmv[:, :, 1], EPS, None, ALU.add).then_inc(ln_steps, 1)

            def x_normalise(b):
                newton([xrs[:, i, :] for i in range(4)], ln_steps, LNSTEPS * b + LNVAR, root_done, b + 1)
                for q in range(QT):
                    last = nc.vector.tensor_scalar(xn[:, q, :], xs[:, bass.ds(QT * b + q, 1), :].rearrange("p o d -> p (o d)"),
                                                   xmv[:, q, 0:1], xrs[:, 2, q:q + 1], ALU.subtract, ALU.mult)
                last.then_inc(xn_done, 1)

            def q_full(b):
                dve.wait_ge(some_in, 16)
                dve.wait_ge(q_ready, b + 1)
                for mt in range(2):
                    nc.vector.tensor_scalar(qf[:, mt, :], S[:, 1, mt * LQ:(mt + 1) * LQ], bq_s[:, mt:mt + 1],
                                            some[:, bass.ds(b, 1)], ALU.add, ALU.mult).then_inc(qf_done, 1)

            def q_rest(b):
                for mt in range(2):
                    dve.wait_ge(qh_done, 2 * b + mt + 1)
                    nc.vector.tensor_tensor(qres[:, mt, :], qf[:, mt, :], qpart[:, mt, 0, :], ALU.subtract
                                            ).then_inc(qres_done, 1)
                for mt in range(2):
                    dve.wait_ge(qm_done, 2 * b + mt + 1)
                    nc.vector.tensor_tensor(qpart[:, mt, 2, :], qres[:, mt, :], qpart[:, mt, 1, :], ALU.subtract
                                            ).then_inc(ql_done, 1)

            dve.wait_ge(cols_in, 16)
            dve.wait_ge(rows_in, 16)
            dve.wait_ge(pads_set, 6)
            def batch(b, final):
                for c in range(CH):
                    if c == 1 and not final:
                        dve.wait_ge(ln_steps, LNSTEPS * (b + 1) + QT)
                    if final and c == 1:
                        maxima_of(first, 0, 0, 0)
                    if final and c == 2:
                        max_rows(first, 0, 0, 0)
                    k_rest(b, c)
                    if c == 1 and not final:
                        x_moments(b + 1)
                    if final and c == 1:
                        maxima_of(first, 0, 0, 1)
                    v_tiles(b, c, final)
                    if c == 0 and isinstance(b, int) and b == 0:
                        x_normalise(0)
                    if c == 0 and not final:
                        x_sums(b + 1)
                if final:
                    dve.wait_ge(v_done, V0 + KT * B)
                    nc.vector.memset(O[:, :, 0:LQ], 0.0).then_inc(o_zeroed, 1)
                q_rest(b)
                if not final:
                    x_normalise(b + 1)


            def moments(mv, tiles, steps):
                for n in tiles:
                    nc.vector.bn_aggr(mv[:, n, :], st[:, n, :]).then_inc(steps, 1)

            def variances(s_, t0, t1, steps):
                dve.wait_ge(s_.rstd_steps, steps)
                nc.vector.tensor_scalar(rs[:, 0, t0:t1], mv2[:, t0:t1, 1], EPS, None, ALU.add).then_inc(s_.var_done, 1)

            def normalise(dst, src, mv, t, done, read):
                if t >= 2:
                    dve.wait_ge(read, KC * (t - 1))
                for i in range(TT):
                    n = TT * t + i
                    nc.vector.tensor_scalar(dst[:, t % 2, i, :], src[:, n, :], mv[:, n, 0:1], rs[:, 2, n:n + 1],
                                            ALU.subtract, ALU.mult).then_inc(done, 1)

            def maxima_of(s_, n, s, h):
                for i, products in enumerate(s_.maxima):
                    use = s_.uses * n + h * len(s_.maxima) + i
                    dve.wait_ge(s_.max_ready, use + 1)
                    if s_ is first:
                        nc.vector.tensor_reduce(mx[:, s % 2, :, h], MB[:, :].rearrange("p (q k) -> p q k", q=QT),
                                                AX.X, ALU.max, negate=True).then_inc(s_.max_taken, 1)
                    else:
                        _, q, k, w = products[0]
                        nc.vector.tensor_reduce(mxp[:, q, h, i % 4:i % 4 + 1], MB[:, 0:w], AX.X, ALU.max
                                                ).then_inc(s_.max_taken, 1)
                if s_ is whole and h == HG - 1:
                    dve.wait_ge(s_.max_taken, ONE + s_.uses * n + HG * len(s_.maxima))
                    nc.vector.tensor_reduce(mx[:, s % 2], mxp[:], AX.X, ALU.max, negate=True
                                            ).then_inc(s_.mx_done, 1)

            def max_rows(s_, n, b, s):
                dve.wait_ge(s_.max_ready, s_.uses * (n + 1))
                dve.wait_ge(s_.mrow_in[(s + 2) % SLOTS], ONE + 16 * 3 * (b if s < 2 else b + 1))
                hi, mi, lo = (mrow[:, s % 2, part, :] for part in range(3))
                nc.vector.tensor_copy(hi, MB[0:HG, 0:LQ]).then_inc(s_.m_steps, 1)
                dve.wait_ge(s_.m_steps, 2 * n + 1)
                nc.vector.tensor_tensor(mres[:], MB[0:HG, 0:LQ], hi, ALU.subtract).then_inc(s_.max_taken, 1)
                dve.wait_ge(s_.max_taken, ONE + s_.uses * (n + 1))
                nc.vector.tensor_copy(mi, mres[:]).then_inc(s_.m_steps, 1)
                dve.wait_ge(s_.m_steps, 2 * n + 2)
                nc.vector.tensor_tensor(lo, mres[:], mi, ALU.subtract).then_inc(s_.mrow_done, 1)

            def take_o(s_, n, s):
                dve.wait_ge(s_.o_ready, ONE + n + 1)
                nc.vector.tensor_copy(osb[:, s % 2, :], O[:, s % 2, 0:LQ]).then_inc(s_.o_taken, 1)

            def divide(s_, b, n, s):
                dve.wait_ge(s_.x_ready, XU * b + s + 1)
                ot = XB[:, 0:QT * P].rearrange("p (q h w) -> p q h w", q=QT, w=32)
                nc.vector.reciprocal(rec[:], ot[:, :, :, HD]).then_inc(s_.rec_done, 1)
                if s_ is first:
                    dve.wait_ge(good_steps, n + 1)
                    nc.vector.scalar_tensor_tensor(out=good[:], in0=ot[:, :, :, HD], scalar=LARGE, in1=good[:],
                                                   op0=ALU.is_lt, op1=ALU.mult).then_inc(good_steps, 1)
                dve.wait_ge(s_.rec_done, n + 1)
                nc.vector.tensor_tensor(
                    att[:, :, s * HG * HD:(s + 1) * HG * HD].rearrange("p q (h d) -> p q h d", d=HD),
                    ot[:, :, :, 0:HD], rec[:].unsqueeze(3).broadcast_to([P, QT, HG, HD]), ALU.mult
                ).then_inc(s_.x_taken, 1)

            def take_att_t(s_, b):
                dve.wait_ge(s_.x_ready, XU * b + SLOTS + 1)
                nc.vector.tensor_copy(attT[:].rearrange("p k q -> p (k q)"), XB[:, :]).then_inc(s_.x_taken, 1)

            def hidden(s_, b):
                dve.wait_ge(s_.x_ready, XU * b + SLOTS + 2)
                rows_ = bass.ds(QT * b, QT)
                nc.vector.tensor_tensor(hid[:, rows_, :], XB[:, :].rearrange("p (q d) -> p q d", q=QT),
                                        xs[:, rows_, :], ALU.add).then_inc(s_.x_taken, 1)
                dve.wait_ge(s_.x_taken, ONE + XU * (b + 1))
                for q in range(QT):
                    last = nc.vector.bn_stats(st[:, bass.ds(QT * b + q, 1), :], hid[:, bass.ds(QT * b + q, 1), :])
                last.then_inc(s_.h_steps, 1)

            def attention(s_, b, start, final):
                for s in range(SLOTS):
                    n = SLOTS * b + s
                    b2 = b if s < 2 else b + 1
                    s2 = (s + 2) % SLOTS
                    before = not (start and s == 0)
                    ahead = s < 2 or not final
                    if start and s == 0:
                        prepare(s_, b, 1)
                    if ahead:
                        maxima_of(s_, n + 2, s2, 0)
                    if before:
                        take_o(s_, n - 1, (s - 1) % SLOTS)
                    if ahead:
                        maxima_of(s_, n + 2, s2, 1)
                    if before:
                        divide(s_, b if s else b - 1, n - 1, (s - 1) % SLOTS)
                    if ahead:
                        maxima_of(s_, n + 2, s2, 2)
                        maxima_of(s_, n + 2, s2, 3)
                    if before and s == 0:
                        take_att_t(s_, b - 1)
                    if ahead:
                        max_rows(s_, n + 2, b2, s2)
                    if before and s == 0:
                        hidden(s_, b - 1)

            def finish(s_, b):
                take_o(s_, SLOTS * (b + 1) - 1, SLOTS - 1)
                divide(s_, b, SLOTS * (b + 1) - 1, SLOTS - 1)
                take_att_t(s_, b)
                if s_ is first:
                    newton(hid_rs(0, HEAD), s_.rstd_steps, HEAD, s_.root_done, 1)
                    dve.wait_ge(mlpw_lo, 1)
                    normalise(yn, hid, mv2, 0, s_.yn0_done, yt_ready)
                hidden(s_, b)

            def prepare(s_, b, s):
                for h in range(HG):
                    maxima_of(s_, SLOTS * b + s, s, h)
                max_rows(s_, SLOTS * b + s, b, s)

            def hid_rs(t0, t1):
                return [rs[:, i, t0:t1] for i in range(4)]

            x_sums(0)
            dve.wait_ge(ln_steps, QT)
            nc.vector.memset(good[:], 1.0).then_inc(good_steps, 1)
            x_moments(0)
            batch(0, False)
            with dve.Fori(1, B - 1) as b:
                batch(b, False)
            batch(B - 1, True)
            dve.wait_ge(xb_done, 1)
            attention(first, 0, True, False)
            with dve.Fori(1, B - 1) as b:
                attention(first, b, False, False)
            attention(first, B - 1, False, True)
            dve.wait_ge(first.h_steps, B - 1)
            moments(mv2, range(HEAD), first.rstd_steps)
            variances(first, 0, HEAD, HEAD)
            finish(first, B - 1)
            dve.wait_ge(first.h_steps, B)
            moments(mv2, range(HEAD, TOK), first.rstd_steps)
            variances(first, HEAD, TOK, TOK + 5)
            dve.wait_ge(good_steps, SLOTS * B + 1)
            nc.vector.tensor_reduce(good_p[:], good[:], AX.XY, ALU.min).then_inc(good_steps, 1)
            dve.wait_ge(good_ready, 1)
            nc.vector.tensor_reduce(good_all[:], MB[0:1, 0:P], AX.X, ALU.min).then_inc(good_steps, 1)
            dve.wait_ge(good_steps, SLOTS * B + 3)
            nc.vector.tensor_copy(flag[:], good_all[:]).then_inc(flag_done, 1)
            newton(hid_rs(HEAD, TOK), first.rstd_steps, TOK + 5, first.root_done, 2)
            with failed(dve):
                with dve.Fori(0, B) as b:
                    prepare(whole, b, 0)
                    attention(whole, b, True, True)
                    finish(whole, b)
                dve.wait_ge(whole.h_steps, B)
                moments(mv2, range(TOK), whole.rstd_steps)
                variances(whole, 0, TOK, TOK)
                newton(hid_rs(0, TOK), whole.rstd_steps, TOK, whole.root_done, 1)
                normalise(yn, hid, mv2, 0, whole.yn0_done, yt_ready)


            def y_high(c):
                dve.wait_ge(yt_done, KC * (c + 1))
                if c >= 2:
                    dve.wait_ge(fc_ready, NI * (c - 1))
                nc.vector.tensor_copy(y_hi[:, c % 2], yT[:, c % 2]).then_inc(yhi_done, 1)

            y_high(0)
            for c in range(NTG):
                for i in range(NI):
                    j = NI * c + i
                    dve.wait_ge(g_done, j + 1)
                    nc.vector.tensor_copy(g_hi[:, i, :], g[:, j % 2, :]).then_inc(ghi_done, 1)
                    dve.wait_ge(ghi_done, j + 1)
                    nc.vector.tensor_tensor(g_lo[:, i, :], g[:, j % 2, :], g_hi[:, i, :].bitcast(F32), ALU.subtract
                                            ).then_inc(glo_done, 1)
                    if i == 1 and c + 1 < NTG:
                        normalise(yn, hid, mv2, c + 1, yn_done, yt_ready)
                    if i == 6 and c + 1 < NTG:
                        y_high(c + 1)
                for t in range(TT):
                    n = TT * c + t
                    dve.wait_ge(pj_ready, n + 1)
                    if n >= 2:
                        dve.wait_ge(out_done[n % 2], 16 * (n // 2))
                    nc.vector.tensor_tensor(ob[:, n % 2, :], O[:, n % 2, 0:D], pjb_s, ALU.add).then_inc(ob_half, 1)
                    dve.wait_ge(ob_half, n + 1)
                    nc.vector.tensor_tensor(ob[:, n % 2, :], ob[:, n % 2, :], hid[:, n, :], ALU.add
                                            ).then_inc(ob_done, 1)

        @block.tensor
        def _(pe):
            def product3(dst, w, m):
                terms = [(a, c) for (wh, wl), (mh, ml) in zip(w, m) for a, c in ((wh, mh), (wh, ml), (wl, mh))]
                for i, (a, c) in enumerate(terms):
                    last = nc.tensor.matmul(dst, a, c, start=i == 0, stop=i == len(terms) - 1)
                return last

            def batch(b, final):
                for c in range(CH):
                    n = NKE[c]
                    pe.wait_ge(lo_done, CH * b + c + 1)
                    if c == CH - 1:
                        pe.wait_ge(idn_in, 16)
                        pe.wait_ge(xn_done, b + 1)
                        pe.wait_ge(kres_done, 2 * CH * b + 2 * CH + 1)
                        for k in range(KC):
                            for q in range(QT):
                                last = nc.tensor.transpose(S[:, 0, k * LQ + q * P:k * LQ + (q + 1) * P],
                                                           xn[:, q, k * P:(k + 1) * P], idn[:])
                        last.then_inc(xt_ready, 1)
                    for mt in range(2):
                        j = 2 * c + mt
                        pe.wait_ge(kres_done, 2 * CH * b + j + 1)
                        if j == 1:
                            pe.wait_ge(qf_done, QF0 + 2 * b)
                        cut = slice(mt * P, (mt + 1) * P)
                        product3(S[:, j % 4, 0:n], [(w_hi[:, 0, k, cut], w_lo[:, 0, k, cut]) for k in range(KC)],
                                 [(c_hi[:, c, k, 0:n], c_lo[:, c, k, 0:n]) for k in range(KC)]
                                 ).then_inc(k_ready, 1)
                        if final and c == 1:
                            if mt == 0:
                                pe.wait_ge(v_done, KT * b + V0 + 3)
                            maxima_of(first, 0, 0, 0, mt)
                        if final and c == 2 and mt == 0:
                            max_rows(first, 0, 0)
                    for t in range(NT[c]):
                        kt = T0[c] + t
                        m = TAIL if kt == KT - 1 else P
                        if final and kt == 6:
                            pe.wait_ge(first.max_taken, ONE + first.uses)
                        pe.wait_ge(v_done, KT * b + (V0 if kt == 0 else kt if kt < 4 else kt + 1))
                        cut = slice(t * P, t * P + m)
                        product3(v_bank(kt)[0:m, 0:D], [(c_hi[:, c, k, cut], c_lo[:, c, k, cut]) for k in range(KC)],
                                 [(w_hi[:, 1, k, :], w_lo[:, 1, k, :]) for k in range(KC)]).then_inc(v_ready, 1)
                        if final and c == 1 and t >= 1:
                            maxima_of(first, 0, 0, 0, t + 1)
                        if c == CH - 1 and t == 0:
                            pe.wait_ge(wqc_in, 16)
                            pe.wait_ge(xt_done, KC * (b + 1))
                            pe.wait_ge(kres_done, 2 * CH * b + 2 * CH + 2)
                            for mt in range(2):
                                for k in range(KC):
                                    last = nc.tensor.matmul(S[:, 1, mt * LQ:(mt + 1) * LQ],
                                                            w_qc_s[:, 0, k, mt * P:(mt + 1) * P], xT[:, k, :],
                                                            start=k == 0, stop=k == KC - 1)
                            last.then_inc(q_ready, 1)

            def turn(dst, src, t, normed, taken, ready):
                for i in range(TT):
                    pe.wait_ge(normed, TT * max(t - 1, 0) + i + 1)
                    for k in range(KC):
                        if t >= 1 and i == 0:
                            pe.wait_ge(taken, KC * (t - 1) + k + 1)
                        last = nc.tensor.transpose(dst[k][:, i * P:(i + 1) * P],
                                                   src[:, t % 2, i, k * P:(k + 1) * P], idn[:])
                        if i == TT - 1:
                            last.then_inc(ready, 1)

            def maxima_of(s_, n, b, s, h):
                if h == 0:
                    pe.wait_ge(s_.slot_in[s], 16 * 8 * (b + 1))
                for i, products in enumerate(s_.maxima):
                    pe.wait_ge(s_.max_taken, ONE + s_.uses * n + h * len(s_.maxima) + i)
                    for col, q, k, w in products:
                        last = nc.tensor.matmul(MB[:, col:col + w], qst[0:MASKROW + 1, s, h, q * P:(q + 1) * P],
                                                kst[0:MASKROW + 1, s, h, k:k + w], start=True, stop=True)
                    last.then_inc(s_.max_ready, 1)

            def max_rows(s_, n, s):
                pe.wait_ge(s_.max_taken, ONE + s_.uses * (n + 1) - 1)
                if s_ is whole:
                    pe.wait_ge(s_.mx_done, n + 1)
                for q in range(QT):
                    last = nc.tensor.matmul(MB[0:HG, q * P:(q + 1) * P], mx[:, s % 2, q, :], idn[:],
                                            start=True, stop=True)
                last.then_inc(s_.max_ready, 1)

            def scores(s_, b, s, kt):
                n = s * KT + kt
                if kt == 0:
                    pe.wait_ge(s_.mrow_in[s], ONE + 16 * 3 * (b + 1))
                pe.wait_ge(s_.exp_done, SLOTS * KT * b + n + 1)
                for h in range(HG):
                    last = nc.tensor.matmul(S[:, 2 * (n % 2) + h // 2, (h % 2) * LQ:(h % 2 + 1) * LQ],
                                            kst[0:KROWS, s, h, kt * P:(kt + 1) * P], qst[0:KROWS, s, h, :],
                                            start=True, stop=True)
                last.then_inc(s_.scores_done, 1)

            def values(s_, b, s, kt):
                if kt == 0:
                    pe.wait_ge(s_.o_taken, SLOTS * b + s + 1)
                for h in range(HG):
                    last = nc.tensor.matmul(O[32 * h:32 * h + VW, s % 2, 0:LQ], vsl[:, s, kt, h * VW:(h + 1) * VW],
                                            pr[:, (s * KT + kt) % PBUF, h * LQ:(h + 1) * LQ],
                                            start=kt == 0, stop=kt == KT - 1, skip_group_check=True)
                if kt == KT - 1:
                    last.then_inc(s_.o_ready, 1)

            def turn_o(s_, b, n, s):
                pe.wait_ge(s_.o_taken, O0 + n + 1)
                pe.wait_ge(s_.x_taken, ONE + XU * b + s)
                for q in range(QT):
                    last = nc.tensor.transpose(XB[:, q * P:(q + 1) * P], osb[:, s % 2, q * P:(q + 1) * P], idn[:])
                last.then_inc(s_.x_ready, 1)

            def turn_att(s_, b):
                pe.wait_ge(s_.x_taken, ONE + XU * b + SLOTS)
                for k in range(KC):
                    for q in range(QT):
                        last = nc.tensor.transpose(XB[:, k * LQ + q * P:k * LQ + (q + 1) * P],
                                                   att[:, q, k * P:(k + 1) * P], idn[:])
                last.then_inc(s_.x_ready, 1)

            def project(s_, b):
                pe.wait_ge(s_.x_taken, ONE + XU * b + SLOTS + 1)
                for q in range(QT):
                    for k in range(KC):
                        last = nc.tensor.matmul(XB[:, q * D:(q + 1) * D], attT[:, k, q * P:(q + 1) * P],
                                                w_qc_s[:, 1, k, :], start=k == 0, stop=k == KC - 1)
                last.then_inc(s_.x_ready, 1)

            def attention(s_, b, start, final):
                for s in range(SLOTS):
                    n = SLOTS * b + s
                    b2 = b if s < 2 else b + 1
                    s2 = (s + 2) % SLOTS
                    before = not (start and s == 0)
                    ahead = s < 2 or not final
                    opening = start and s == 0
                    steps, rows_step = (OPENSTEPS, KT - 2) if opening else (MAXSTEPS, 9)
                    for kt in range(KT):
                        scores(s_, b, s, kt)
                        if opening and kt < HG:
                            maxima_of(s_, n + 1, b, 1, kt)
                        if opening and kt == HG:
                            max_rows(s_, n + 1, 1)
                        if ahead and kt in steps:
                            maxima_of(s_, n + 2, b2, s2, steps.index(kt))
                        if before and kt == 4:
                            turn_o(s_, b if s else b - 1, n - 1, (s - 1) % SLOTS)
                        if before and s == 0 and kt == 8:
                            turn_att(s_, b - 1)
                        if ahead and kt == rows_step:
                            max_rows(s_, n + 2, s2)
                        if before and s == 0 and kt == 11:
                            project(s_, b - 1)
                        if kt >= LAG:
                            values(s_, b, s, kt - LAG)
                        elif before:
                            values(s_, b if s else b - 1, (s - 1) % SLOTS, KT + kt - LAG)

            def finish(s_, b):
                for kt in range(KT - LAG, KT):
                    pe.wait_ge(s_.exp_done, EXP0 + SLOTS * KT * (b + 1) - KT + kt + 1)
                    values(s_, b, SLOTS - 1, kt)
                turn_o(s_, b, SLOTS * (b + 1) - 1, SLOTS - 1)
                turn_att(s_, b)
                project(s_, b)

            def prepare(s_, b):
                for h in range(HG):
                    maxima_of(s_, SLOTS * b, b, 0, h)
                max_rows(s_, SLOTS * b, 0)

            pe.sem_inc(first.o_ready, ONE)
            pe.sem_inc(whole.o_ready, ONE)
            pe.wait_ge(w_split, 2)
            with pe.Fori(0, B - 1) as b:
                batch(b, False)
            batch(B - 1, True)
            pe.wait_ge(v_done, V0 + KT * B)
            pe.wait_ge(kres_done, KRES0 + 2 * CH * B)
            pe.wait_ge(qf_done, QF0 + 2 * B)
            pe.wait_ge(o_zeroed, 1)
            attention(first, 0, True, False)
            with pe.Fori(1, B - 1) as b:
                attention(first, b, False, False)
            attention(first, B - 1, False, True)
            finish(first, B - 1)
            pe.wait_ge(first.max_taken, ONE + first.uses * SLOTS * B)
            pe.wait_ge(good_steps, SLOTS * B + 2)
            nc.tensor.matmul(MB[0:1, 0:P], good_p[:], idn[:], start=True, stop=True).then_inc(good_ready, 1)
            with failed(pe):
                with pe.Fori(0, B) as b:
                    prepare(whole, b)
                    attention(whole, b, True, True)
                    finish(whole, b)
                pe.wait_ge(whole.max_taken, ONE + whole.uses * SLOTS * B)
                pe.wait_ge(whole.x_taken, ONE + XU * B)
                pe.wait_ge(whole.yn0_done, TT)

            pe.wait_ge(mlpw_lo, 2)
            pe.wait_ge(first.x_taken, ONE + XU * B)
            pe.wait_ge(flag_done, 1)
            turn((MB[:, :], XB[:, :]), yn, 0, first.yn0_done, yt_done, yt_ready)
            for c in range(NTG):
                pe.wait_ge(ylo_done, c + 1)
                for i in range(NI):
                    j = NI * c + i
                    if j >= 4:
                        pe.wait_ge(g_done, j - 3)
                    cut = slice(i * P, (i + 1) * P)
                    product3(S[:, j % 4, :], [(fc_hi[:, k, cut], fc_lo[:, k, cut]) for k in range(KC)],
                             [(y_hi[:, c % 2, k, :], y_lo[:, c % 2, k, :]) for k in range(KC)]).then_inc(fc_ready, 1)
                    if i == 3 and c + 1 < NTG:
                        turn((MB[:, :], XB[:, :]), yn, c + 1, yn_done, yt_done, yt_ready)
                for t in range(TT):
                    n = TT * c + t
                    if n >= 2:
                        pe.wait_ge(ob_half, n - 1)
                    for i in range(NI):
                        if t == 0:
                            pe.wait_ge(glo_done, NI * c + i + 1)
                        cut = slice(t * P, (t + 1) * P)
                        for m, (w, v) in enumerate(((g_hi, pj_hi), (g_hi, pj_lo), (g_lo, pj_hi))):
                            last = nc.tensor.matmul(O[:, n % 2, 0:D], w[:, i, cut], v[:, i, :],
                                                    start=i == 0 and m == 0, stop=i == NI - 1 and m == 2)
                    last.then_inc(pj_ready, 1)


def kernel(x, ctx_2048, mask_BxS2_bf1, **w):
    import concourse.bacc as bacc
    from concourse.bass_utils import run_bass_kernel_spmd

    w = {n.removeprefix("L0_xattn_"): np.asarray(a) for n, a in w.items()}
    con = np.ascontiguousarray

    def chunks(a):
        return a.reshape(-1, P, a.shape[-1]).transpose(1, 0, 2)

    def by_width(a):
        return a.reshape(*a.shape[:-1], 2, HM, HD).swapaxes(-1, -2).reshape(a.shape)

    def column(a):
        return a.reshape(-1, P).T

    arrays = {
        "x": con(np.asarray(x).reshape(TOK, P, D)),
        "ctx_t": con(np.asarray(ctx_2048).transpose(0, 2, 1).reshape(B, KC, P, LK)),
        "mask": con(np.asarray(mask_BxS2_bf1)).view(np.uint8),
        "w_kv": con(np.stack([chunks(by_width(w["k_w"])), chunks(w["v_w"])], 1)),
        "w_qc": con(np.stack([chunks(by_width(w["q_w"])), chunks(w["cproj_w"])], 1)),
        "fc": con(chunks(w["fc_w"])),
        "pj": con(chunks(w["proj_w"])),
        "cols": con(np.concatenate([column(a) for a in (
            w["ln1_w"], w["ln1_b"], w["ln2_w"], w["ln2_b"], by_width(w["q_b"]), by_width(w["k_b"]), w["fc_b"])], 1)),
        "rows": con(np.stack([w["v_b"], w["cproj_b"], w["proj_b"]])),
        "ident": np.eye(P, dtype=np.float32),
    }
    nc = bacc.Bacc("TRN2", target_bir_lowering=False, num_devices=1)
    aps = {n: nc.dram_tensor(f"in_{n}", a.shape, mybir.dt.from_np(a.dtype), kind="ExternalInput").ap()
           for n, a in arrays.items()}
    out = nc.dram_tensor("out", [B * LQ, D], F32, kind="ExternalOutput").ap()
    build(nc, out=out, **aps)
    r = run_bass_kernel_spmd(nc, [{f"in_{n}": a for n, a in arrays.items()}], core_ids=[0])
    return r.results[0]["out"].reshape(B, LQ, D)
```
